# Optimizing a Trainium2 kernel written in Bass

```python
import numpy as np
import jax
import jax.numpy as jnp

def _softmax(x, axis=-1):
    return jax.nn.softmax(x, axis=axis)

def _gelu(x):
    return jax.nn.gelu(x, approximate=True)

def _silu(x):
    return jax.nn.silu(x)

def _sigmoid(x):
    return jax.nn.sigmoid(x)

def _layernorm(x, axis=-1, eps=1e-05):
    m = jnp.mean(x, axis=axis, keepdims=True)
    v = jnp.var(x, axis=axis, keepdims=True)
    return (x - m) / jnp.sqrt(v + eps)

def _scatter_add(tgt, idx, src, axis=0):
    return tgt.at[idx].add(src)

def _segment_sum(src, seg, n):
    return jax.ops.segment_sum(src, seg, n)
kernel_name = 'mk_gnn_preln_d1_gnn_r8_144f44'

def setup_inputs(seed: int=0):
    np.random.seed(seed)
    _w = jnp.asarray

    def _rec_inputs():
        import jax
        import jax.numpy as jnp
        _gk = jax.random.key(seed)
        x = -0.000202 + 1 * jax.random.normal(jax.random.fold_in(_gk, 1), (12500, 64), jnp.float32)
        src = jax.random.randint(jax.random.fold_in(_gk, 2), (200000,), 0, 12500, jnp.int32)
        dst = jnp.minimum((12500 * jax.random.uniform(jax.random.fold_in(_gk, 3), (200000,)) ** 2.0).astype(jnp.int32), 99999)
        _o = jnp.argsort(dst, stable=True)
        src = src[_o]
        dst = dst[_o]
        edge_attr_64 = 0.000189758 + 1.00013 * jax.random.normal(jax.random.fold_in(_gk, 11), (200000, 64), jnp.float32)
        return (x, src, dst, edge_attr_64)
    x, src, dst, edge_attr_64 = _rec_inputs()

    def _L0_gnn_setup():
        import jax, jax.numpy as jnp
        import numpy as np
        N_NODES = 12500
        N_EDGES = 100000
        DIM = 64
        HEADS = 4
        HEAD_DIM = DIM // HEADS
        ALPHA = 0.1
        K_ITERS = 8

        def _mapr(x, edge_index, edge_attr, Wq, Wk, Wv, We):
            N = x.shape[0]
            src, dst = (edge_index[0], edge_index[1])
            q = (x @ Wq).reshape(N, HEADS, HEAD_DIM)
            k = (x @ Wk).reshape(N, HEADS, HEAD_DIM)
            v = (x @ Wv).reshape(N, HEADS, HEAD_DIM)
            e = (edge_attr @ We).reshape(-1, HEADS, HEAD_DIM)
            logits = jnp.sum(q[dst] * (k[src] + e), axis=-1) / np.sqrt(HEAD_DIM)
            m = jax.ops.segment_max(logits, dst, num_segments=N)
            ex = jnp.exp(logits - m[dst])
            denom = jax.ops.segment_sum(ex, dst, num_segments=N)
            att = ex / (denom[dst] + 1e-16)

            def step(z, _):
                msg = att[:, :, None] * z[src]
                agg = jax.ops.segment_sum(msg, dst, num_segments=N)
                return (ALPHA * v + (1.0 - ALPHA) * agg, None)
            z, _ = jax.lax.scan(step, v, None, length=K_ITERS)
            return z.reshape(N, DIM)
        key = jax.random.key(seed)
        ks = jax.random.split(key, 7)
        x = jax.random.normal(ks[0], (N_NODES, DIM), dtype=jnp.float32)
        edge_index = jax.random.randint(ks[1], (2, N_EDGES), 0, N_NODES, dtype=jnp.int64)
        edge_attr = jax.random.normal(ks[2], (N_EDGES, DIM), dtype=jnp.float32)
        s = 1.0 / np.sqrt(DIM)
        Wq = jax.random.normal(ks[3], (DIM, DIM), dtype=jnp.float32) * s
        Wk = jax.random.normal(ks[4], (DIM, DIM), dtype=jnp.float32) * s
        Wv = jax.random.normal(ks[5], (DIM, DIM), dtype=jnp.float32) * s
        We = jax.random.normal(ks[6], (DIM, DIM), dtype=jnp.float32) * s
        return {'x': x, 'edge_index': edge_index, 'edge_attr': edge_attr, 'Wq': Wq, 'Wk': Wk, 'Wv': Wv, 'We': We}
    _L0_gnn_all = _L0_gnn_setup()
    _L0_gnn_in = {k: v for k, v in _L0_gnn_all.items() if k in ('Wq', 'Wk', 'Wv', 'We')}
    del _L0_gnn_all
    return {'x': x, 'src': src, 'dst': dst, 'edge_attr_64': edge_attr_64, 'L0_gnn_Wq': _L0_gnn_in['Wq'], 'L0_gnn_Wk': _L0_gnn_in['Wk'], 'L0_gnn_Wv': _L0_gnn_in['Wv'], 'L0_gnn_We': _L0_gnn_in['We']}

def reference(x, src, dst, edge_attr_64, L0_gnn_Wq, L0_gnn_Wk, L0_gnn_Wv, L0_gnn_We):
    import jax
    import jax.numpy as jnp

    def _L0_gnn_ref(x, edge_index, edge_attr, Wq, Wk, Wv, We):
        import jax, jax.numpy as jnp
        import numpy as np
        N_NODES = 12500
        N_EDGES = 100000
        DIM = 64
        HEADS = 4
        HEAD_DIM = DIM // HEADS
        ALPHA = 0.1
        K_ITERS = 8

        def _mapr(x, edge_index, edge_attr, Wq, Wk, Wv, We):
            N = x.shape[0]
            src, dst = (edge_index[0], edge_index[1])
            q = (x @ Wq).reshape(N, HEADS, HEAD_DIM)
            k = (x @ Wk).reshape(N, HEADS, HEAD_DIM)
            v = (x @ Wv).reshape(N, HEADS, HEAD_DIM)
            e = (edge_attr @ We).reshape(-1, HEADS, HEAD_DIM)
            logits = jnp.sum(q[dst] * (k[src] + e), axis=-1) / np.sqrt(HEAD_DIM)
            m = jax.ops.segment_max(logits, dst, num_segments=N)
            ex = jnp.exp(logits - m[dst])
            denom = jax.ops.segment_sum(ex, dst, num_segments=N)
            att = ex / (denom[dst] + 1e-16)

            def step(z, _):
                msg = att[:, :, None] * z[src]
                agg = jax.ops.segment_sum(msg, dst, num_segments=N)
                return (ALPHA * v + (1.0 - ALPHA) * agg, None)
            z, _ = jax.lax.scan(step, v, None, length=K_ITERS)
            return z.reshape(N, DIM)
        h = _mapr(x, edge_index, edge_attr, Wq, Wk, Wv, We)
        h = jax.nn.relu(h)
        return x + h
    edge_index = jnp.stack([src, dst])
    h = jnp.maximum(_layernorm(x, axis=-1), 0.0)
    x = x + _L0_gnn_ref(h, edge_index, edge_attr_64, L0_gnn_Wq, L0_gnn_Wk, L0_gnn_Wv, L0_gnn_We)
    return x

_drawn_inputs = setup_inputs


def setup_inputs(seed=0):
    import zlib

    import numpy as np

    out = dict(_drawn_inputs(seed))
    spreads = {}
    factors = {'edge_attr_64': 8.0, 'L0_gnn_Wq': 6.769, 'L0_gnn_Wk': 8.0, 'L0_gnn_We': 8.0}
    for name, (base, spread) in spreads.items():
        noise = np.random.default_rng([zlib.crc32(name.encode()), seed]).standard_normal(out[name].shape)
        drawn = base * np.exp(spread * noise) if base else spread * noise
        out[name] = jnp.asarray(drawn.astype(out[name].dtype))
    for name, factor in factors.items():
        out[name] = (out[name] * factor).astype(out[name].dtype)
    return out
```

```python
import numpy as np
import concourse.bass as bass
from concourse import mybir
from contextlib import ExitStack

P = 128
N_NODES = 12500
N_EDGES = 200000
DIM = 64
HEADS = 4
HD = DIM // HEADS
K_ITERS = 8
ALPHA = 0.1
LN_EPS = 1e-05
NB = -(-N_NODES // P)
PAD_NODE = NB * P - 1
TILES = 4
GE = TILES * P
U = 4
BODIES = -(-N_EDGES // (GE * U))
G = BODIES * U
NT = G * TILES
SUB = 32
NSB = NB * P // SUB
AW = DIM + HEADS
BIG = 2.0 ** 100
M_INIT = -(2.0 ** 120)
SCALE = 1.0 / HD ** 0.5


def build_gnn(nc, x, src, dst, dst_rows, dst_minmax, ea_t, wq, wk, wv, we, out):
    fp32, bf16, i32 = mybir.dt.float32, mybir.dt.bfloat16, mybir.dt.int32
    ALU, ACT, AX = mybir.AluOpType, mybir.ActivationFunctionType, mybir.AxisListType

    with ExitStack() as ctx:
        def sb(name, shape, dt=fp32):
            return ctx.enter_context(nc.sbuf_tensor(name, shape, dt))

        def pb(name, shape, dt=fp32):
            return ctx.enter_context(nc.psum_tensor(name, shape, dt))

        def sem(name):
            return ctx.enter_context(nc.semaphore(name))

        def sems(name, n):
            return [sem(f"{name}{i}") for i in range(n)]

        kv_table = nc.dram_tensor("kv_table", [P * NB, 2 * DIM], fp32, kind="Internal").ap()
        z_table = nc.dram_tensor("z_table", [P * NB, DIM], fp32, kind="Internal").ap()
        vsrc = nc.dram_tensor("vsrc", [G, P, TILES * DIM], fp32, kind="Internal").ap()
        xh_dram = nc.dram_tensor("xh_dram", [P, NB * DIM], fp32, kind="Internal").ap()
        range_dram = nc.dram_tensor("range_dram", [BODIES, U * 4], i32, kind="Internal").ap()

        r_x = sb("r_x", [P, NB * DIM])
        r_h = sb("r_h", [P, NB * DIM])
        r_q = sb("r_q", [P, NB * DIM])
        r_v = sb("r_v", [P, NB * DIM])
        r_kv = sb("r_kv", [P, NB * 2 * DIM])
        x_v = r_x[:, :].rearrange("p (b d) -> p b d", d=DIM)
        h_v = r_h[:, :].rearrange("p (b d) -> p b d", d=DIM)
        q_sb = r_q[:, :].rearrange("p (b d) -> p b d", d=DIM)
        av = r_v[:, :].rearrange("p (b d) -> p b d", d=DIM)
        kv_sb = r_kv[:, :].rearrange("p (b d) -> p b d", d=2 * DIM)
        assert NT * HEADS == NB * DIM
        weights = r_x
        agg = r_kv[:, 0:NB * AW].rearrange("p (b d) -> p b d", d=AW)
        ring0 = NB * AW
        gather_ring = [r_kv[:, ring0 + u * TILES * 2 * DIM:ring0 + (u + 1) * TILES * 2 * DIM] for u in range(U)]
        ea0 = ring0 + U * TILES * 2 * DIM
        ea_slot = [r_kv[0:DIM, ea0 + u * GE:ea0 + (u + 1) * GE] for u in range(U)]
        assert ea0 + U * GE <= NB * 2 * DIM
        kv_slot = [g.rearrange("p (t d) -> p t d", d=2 * DIM) for g in gather_ring]
        z_slot = [g[:, 0:TILES * DIM].rearrange("p (t d) -> p t d", d=DIM) for g in gather_ring]
        raw = r_q[:, :].bitcast(i32)
        dst_i, src_i = raw[:, 0:NT], raw[:, NT:2 * NT + U * TILES]
        src_lo = raw[:, 2 * NT + U * TILES:3 * NT + 2 * U * TILES]
        minmax_i = r_h[0:BODIES, 0:U * GE].bitcast(i32).rearrange("p (u e) -> p u e", u=U)
        h_sq = r_kv[:, 0:NB * DIM]

        idx_all = sb("idx_all", [P, NT + U * TILES], i32)
        dst_f = sb("dst_f", [P, NT])
        w_qkv = sb("w_qkv", [P, 3 * DIM])
        w_e = sb("w_e", [DIM, DIM])
        iota_i = sb("iota_i", [P, P], i32)
        iota_f = sb("iota_f", [P, P])
        node_i = sb("node_i", [P, NB], i32)
        neg_node = sb("neg_node", [P, NB])
        base_f = sb("base_f", [P, NB])
        part_f = sb("part_f", [P, 1])
        sub_i = sb("sub_i", [P, NSB], i32)
        psub_i = sb("psub_i", [P, 1], i32)
        psub_f = sb("psub_f", [P, 1])
        neg_sub = sb("neg_sub", [P, NSB])
        ident = sb("ident", [P, P])
        neg_ident = sb("neg_ident", [P, P], bf16)
        head_i = sb("head_i", [HEADS, P], i32)
        head_rows = sb("head_rows", [HEADS, P])
        place = sb("place", [P, HEADS, P + 3 * SUB])
        zero_bf = sb("zero_bf", [1, 2 * P], bf16)
        range_i = sb("range_i", [BODIES, U, 4], i32)
        ranges = sb("ranges", [1, G * 4], i32)
        ln_sum = sb("ln_sum", [P, NB])
        ln_r = sb("ln_r", [P, NB])
        eps_col = sb("eps_col", [P, 1])
        h_stage = sb("h_stage", [P, 2 * DIM])
        h_t = sb("h_t", [P, P])
        idx_slot = [sb(f"idx_slot{u}", [P, TILES], i32) for u in range(U)]
        dstb_slot = [sb(f"dstb_slot{u}", [P, GE], i32) for u in range(U)]
        dist = sb("dist", [P, GE], bf16)
        hot_ne = sb("hot_ne", [P, GE])
        hot_en = sb("hot_en", [P, TILES, P])
        mask = sb("mask", [P, 2, GE], bf16)
        q_edge = sb("q_edge", [P, TILES * DIM])
        prod = sb("prod", [P, TILES * DIM])
        lg = sb("lg", [P, TILES * HEADS])
        lg_t = sb("lg_t", [HEADS, GE])
        gmax = sb("gmax", [P, 2])
        m_sub = sb("m_sub", [P, NSB])
        m_node = sb("m_node", [P, NB, HEADS])
        delta = sb("delta", [P, TILES * HEADS])
        msg = [sb(f"msg{u}", [P, TILES, AW]) for u in range(2)]
        r_den = sb("r_den", [P, NB, HEADS])

        ps_a = pb("ps_a", [P, 512])
        ps_q = pb("ps_q", [P, 512])
        ps_t = pb("ps_t", [P, 512])
        ps_b = pb("ps_b", [P, 2, 512])
        ps_w = pb("ps_w", [P, 2, 512])
        EW = TILES * DIM

        x_loaded, w_loaded, idx_loaded, minmax_loaded = sem("x_loaded"), sem("w_loaded"), sem("idx_loaded"), sem("minmax_loaded")
        ranges_ready, ranges_out, ranges_loaded = sem("ranges_ready"), sem("ranges_out"), sem("ranges_loaded")
        iotas_ready, consts_ready, idx_ready = sem("iotas_ready"), sem("consts_ready"), sem("idx_ready")
        dve_step = sem("dve_step")
        centred, squared, var_ready, std_ready, h_ready, xh_ready = (sem(n) for n in (
            "centred", "squared", "var_ready", "std_ready", "h_ready", "xh_ready"))
        h_staged, h_turned, h_t_ready, qkv_done, kv_kept = (sem(n) for n in (
            "h_staged", "h_turned", "h_t_ready", "qkv_done", "kv_kept"))
        kv_stored, xh_stored, xh_loaded = sem("kv_stored"), sem("xh_stored"), sem("xh_loaded")
        idx_in_slot = sem("idx_in_slot")
        gathered, ea_loaded, dstb_loaded = sems("gathered", U), sems("ea_loaded", U), sems("dstb_loaded", U)
        vsrc_stored, vsrc_loaded = sems("vsrc_stored", U), sems("vsrc_loaded", U)
        dstb_used = sem("dstb_used")
        dist_done, hot_ready, hot_used = sem("dist_done"), sem("hot_ready"), sem("hot_used")
        ke_done, q_done, q_ready = sem("ke_done"), sem("q_done"), sem("q_ready")
        prod_done, lg_ready, lg_kept, lgt_done, lgt_ready = sem("prod_done"), sem("lg_ready"), sem("lg_kept"), sem("lgt_done"), sem("lgt_ready")
        mask_ready = sem("mask_ready")
        max_psum, gmax_done = sem("max_psum"), sem("gmax_done")
        m_sub_ready, m_sub_done, m_moved, m_ready = sem("m_sub_ready"), sem("m_sub_done"), sem("m_moved"), sem("m_ready")
        me_done, delta_ready, exp_ready = sem("me_done"), sem("delta_ready"), sem("exp_ready")
        msg_ready = sem("msg_ready")
        hot_en_ready, agg_psum, added = sem("hot_en_ready"), sem("agg_psum"), sem("added")
        r_den_step = sem("r_den_step")
        z_scaled, z_ready, agg_zeroed, z_stored = sem("z_scaled"), sem("z_ready"), sem("agg_zeroed"), sem("z_stored")
        out_ready, out_stored = sem("out_ready"), sem("out_stored")

        SAFE = "the ranges are made on the chip from dst, which are nodes"
        BLOCKS, SUBS = 0, 1
        KV_CHUNK = 7
        KV_STORES = NB // 2 // KV_CHUNK
        EH = TILES * HEADS

        def group0(r, u):
            return r * U + (u - U)

        def group1(r, u):
            return r * U + (u - U + 1)

        def load_range(eng, r, u, which):
            _, v = nc.values_load_multi_w_load_instructions(
                ranges[0:1, bass.ds(group0(r, u) * 4 + 2 * which, 2)], engines=[eng.engine], min_val=0,
                max_val=NSB if which == SUBS else NB, skip_runtime_bounds_check_because=SAFE)
            return v

        def counter(eng, name, start=1):
            c = eng.alloc_register(name)
            eng.reg_mov(c, start)
            return c

        def wait_next(eng, semaphore, c, by=1):
            eng.wait_ge(semaphore, eng.snap(c))
            eng.reg_add(c, c, by)

        def group_weights(g):
            return weights[:, bass.ds(g * EH, EH)]

        block = ctx.enter_context(nc.Block())

        @block.sync
        def _(sp):
            sp.dma_start(r_x[:, :], x).then_inc(x_loaded, 16)
            sp.dma_start(minmax_i, dst_minmax).then_inc(minmax_loaded, 16)
            sp.dma_start(dst_i, dst).then_inc(idx_loaded, 16)
            sp.dma_start(src_i, src).then_inc(idx_loaded, 16)
            for half in range(2):
                for n, w in enumerate((wq, wk, wv)):
                    sp.dma_start(w_qkv[half * DIM:(half + 1) * DIM, n * DIM:(n + 1) * DIM], w).then_inc(w_loaded, 16)
            sp.dma_start(w_e[:, :], we).then_inc(w_loaded, 16)
            sp.wait_ge(ranges_ready, 1)
            sp.dma_start(range_dram, range_i[:, :, :].rearrange("p u a -> p (u a)")).then_inc(ranges_out, 16)
            sp.wait_ge(ranges_out, 16)
            sp.dma_start(ranges[:, :], range_dram.rearrange("b c -> (b c)").unsqueeze(0)).then_inc(ranges_loaded, 16)
            sp.wait_ge(xh_ready, 1)
            sp.dma_start(xh_dram, r_x[:, :]).then_inc(xh_stored, 16)
            kv_rows = kv_table.rearrange("(p b) d -> p b d", b=NB)
            for c in range(KV_STORES):
                sp.wait_ge(kv_kept, (c + 1) * KV_CHUNK)
                cols = slice(2 * c * KV_CHUNK, 2 * (c + 1) * KV_CHUNK)
                sp.dma_start(kv_rows[:, cols, :], kv_sb[:, cols, :]).then_inc(kv_stored, 16)

            sp.wait_ge(kv_stored, 16 * KV_STORES)
            with sp.Fori(1, BODIES + 1) as r:
                for u in range(U):
                    sp.wait_ge(ke_done, group1(r, u))
                    sp.dma_start(ea_slot[u][:, :], ea_t[bass.ds(group0(r, u), 1), :, :].rearrange("a d e -> (a d) e")).then_inc(ea_loaded[u], 16)
                    sp.wait_ge(dstb_used, group1(r, u))
                    sp.dma_start(dstb_slot[u][:, :], dst_rows[bass.ds(group0(r, u), 1), :].broadcast_to([P, GE])).then_inc(dstb_loaded[u], 16)
                for u in range(U):
                    sp.wait_ge(gathered[u], r * (16 * TILES))
                    sp.dma_start(vsrc[bass.ds(group0(r, u), 1), :, :].rearrange("a p (t d) -> (a p) t d", d=DIM),
                                 kv_slot[u][:, :, DIM:2 * DIM]).then_inc(vsrc_stored[u], 16)

            for u in range(U):
                sp.wait_ge(vsrc_stored[u], BODIES * 16)
            sp.wait_ge(ke_done, G + U)
            with sp.Fori(1, BODIES + 1) as r:
                for u in range(U):
                    sp.wait_ge(dstb_used, group1(r, u) + G)
                    sp.dma_start(dstb_slot[u][:, :], dst_rows[bass.ds(group0(r, u), 1), :].broadcast_to([P, GE])).then_inc(dstb_loaded[u], 16)
                    sp.wait_ge(msg_ready, group1(r, u))
                    sp.dma_start(gather_ring[u][:, 0:TILES * DIM], vsrc[bass.ds(group0(r, u), 1), :, :].rearrange("a p e -> (a p) e")).then_inc(vsrc_loaded[u], 16)

            sp.wait_ge(xh_stored, 16)
            sp.wait_ge(q_done, G)
            sp.dma_start(r_q[:, :], xh_dram).then_inc(xh_loaded, 16)
            z_rows = z_table.rearrange("(p b) d -> p (b d)", b=NB)
            with sp.Fori(1, K_ITERS) as it:
                sp.wait_ge(z_ready, it)
                sp.dma_start(z_rows, r_h[:, :]).then_inc(z_stored, 16)
            sp.wait_ge(out_ready, 1)
            sp.dma_start(out, r_h[:, :]).then_inc(out_stored, 16)
            sp.wait_ge(z_stored, 16 * (K_ITERS - 1))
            sp.wait_ge(out_stored, 16)

        @block.gpsimd
        def _(pool):
            nc.gpsimd.iota(iota_i[:, :], [[1, P]], base=0, channel_multiplier=0).then_inc(iotas_ready, 1)
            nc.gpsimd.iota(node_i[:, :], [[P, NB]], base=0, channel_multiplier=1).then_inc(iotas_ready, 1)
            nc.gpsimd.iota(sub_i[:, :], [[SUB, NSB]], base=0, channel_multiplier=0).then_inc(iotas_ready, 1)
            nc.gpsimd.iota(psub_i[:, :], [[0, 1]], base=0, channel_multiplier=1).then_inc(iotas_ready, 1)
            nc.gpsimd.memset(place[:, :, :], 0.0).then_inc(iotas_ready, 1)
            nc.gpsimd.memset(zero_bf[:, :], 0.0).then_inc(iotas_ready, 1)
            nc.gpsimd.memset(m_sub[:, :], M_INIT).then_inc(iotas_ready, 1)
            nc.gpsimd.memset(eps_col[:, :], LN_EPS).then_inc(iotas_ready, 1)

            pool.wait_ge(kv_stored, 16 * KV_STORES)
            group = counter(pool, "pool_group")
            with pool.Fori(1, BODIES + 1):
                for u in range(U):
                    wait_next(pool, idx_in_slot, group)
                    for t in range(TILES):
                        pool.indirect_dma_start(
                            out=kv_slot[u][:, t, :], out_offset=None, in_=kv_table,
                            in_offset=bass.IndirectOffsetOnAxis(ap=idx_slot[u][:, t:t + 1], axis=0)).then_inc(gathered[u], 16)

            nc.gpsimd.memset(agg, 0.0).then_inc(agg_zeroed, 1)

            z_read = counter(pool, "pool_z_read")
            z_in_dram = counter(pool, "pool_z_in_dram", 16)
            with pool.Fori(1, K_ITERS):
                wait_next(pool, z_scaled, z_read)
                nc.gpsimd.memset(agg, 0.0).then_inc(agg_zeroed, 1)
                wait_next(pool, z_stored, z_in_dram, 16)
                with pool.Fori(1, BODIES + 1):
                    for u in range(U):
                        wait_next(pool, idx_in_slot, group)
                        for t in range(TILES):
                            pool.indirect_dma_start(
                                out=z_slot[u][:, t, :], out_offset=None, in_=z_table,
                                in_offset=bass.IndirectOffsetOnAxis(ap=idx_slot[u][:, t:t + 1], axis=0)).then_inc(gathered[u], 16)

        @block.scalar
        def _(act):
            act.wait_ge(centred, 1)
            nc.scalar.activation(h_sq, r_v[:, :], ACT.Square).then_inc(squared, 1)
            act.wait_ge(var_ready, 1)
            act.wait_ge(iotas_ready, 8)
            nc.scalar.activation(ln_sum[:, :], ln_sum[:, :], ACT.Sqrt, bias=eps_col[:, 0:1], scale=1.0 / DIM).then_inc(std_ready, 1)
            act.wait_ge(h_ready, 1)
            with act.Fori(0, NB // 2) as j:
                nc.scalar.activation(h_stage[:, :], r_h[:, bass.ds(j * (2 * DIM), 2 * DIM)], ACT.Copy).then_inc(h_staged, 1)
                act.wait_ge(h_turned, j + 1)
            act.wait_ge(idx_ready, 1)
            for u in range(U):
                nc.scalar.activation(idx_slot[u][:, :], idx_all[:, u * TILES:(u + 1) * TILES], ACT.Copy).then_inc(idx_in_slot, 1)
            act.sem_inc(dstb_used, U)

            act.wait_ge(ranges_loaded, 16)
            act.wait_ge(consts_ready, 1)
            pair = counter(act, "act_pair")
            submask = counter(act, "act_submask")

            def hot_pairs(r, u):
                lo, hi = load_range(act, r, u, BLOCKS)
                with act.Fori(lo, hi) as b:
                    n = act.snap(pair)
                    wait_next(act, hot_used, pair)
                    nc.scalar.activation(dist[:, :], dstb_slot[u][:, :], ACT.Abs, bias=neg_node[:, bass.ds(b, 1)]).then_inc(dist_done, 1)
                    act.wait_ge(dist_done, n)
                    nc.scalar.activation(hot_ne[:, :], dist[:, :], ACT.Relu, bias=1.0, scale=-1.0).then_inc(hot_ready, 1)

            def next_indices(r, u):
                act.wait_ge(idx_ready, 1)
                nc.scalar.activation(idx_slot[u][:, :], idx_all[:, bass.ds(group0(r + 1, u) * TILES, TILES)], ACT.Copy).then_inc(idx_in_slot, 1)

            def p1_hot(r, u):
                act.wait_ge(dstb_loaded[u], r * 16)
                hot_pairs(r, u)

            def p1_q(r, u):
                act.wait_ge(q_done, group1(r, u))
                nc.scalar.activation(q_edge[:, :], ps_q[:, 0:TILES * DIM], ACT.Copy).then_inc(q_ready, 1)

            def p1_masks(r, u):
                act.wait_ge(max_psum, act.snap(submask) + 1)
                act.wait_ge(lgt_done, group1(r, u))
                nc.scalar.activation(lg_t[:, :], ps_t[0:HEADS, :], ACT.Copy).then_inc(lgt_ready, 1)
                lo, hi = load_range(act, r, u, SUBS)
                with act.Fori(lo, hi) as c:
                    n = act.snap(submask)
                    act.wait_ge(max_psum, n)
                    act.reg_add(submask, submask, 1)
                    nc.scalar.activation(mask[:, bass.ds(n % 2, 1), :].rearrange("p a e -> p (a e)"), dstb_slot[u][:, :], ACT.Abs,
                                         bias=neg_sub[:, bass.ds(c, 1)]).then_inc(mask_ready, 1)
                act.wait_ge(mask_ready, act.snap(submask) - 1)
                act.sem_inc(dstb_used, 1)

            def p1_indices(r, u):
                act.wait_ge(gathered[u], r * (16 * TILES))
                act.wait_ge(vsrc_stored[u], r * 16)
                act.wait_ge(ke_done, group1(r, u) + U)
                next_indices(r, u)

            p1_hot(1, 0)
            p1_q(1, 0)
            with act.Fori(1, BODIES) as r:
                for u in range(U):
                    nxt = (r, u + 1) if u + 1 < U else (r + 1, 0)
                    p1_hot(*nxt)
                    p1_masks(r, u)
                    p1_q(*nxt)
                    p1_indices(r, u)
            for u in range(U):
                if u + 1 < U:
                    p1_hot(BODIES, u + 1)
                p1_masks(BODIES, u)
                if u + 1 < U:
                    p1_q(BODIES, u + 1)
                p1_indices(BODIES, u)

            act.wait_ge(m_moved, 1)
            nc.scalar.activation(m_node[:, :, :].rearrange("p b h -> p h b"),
                                 ps_w[:, 0, 0:HEADS * NB].rearrange("p (h b) -> p h b", h=HEADS), ACT.Copy).then_inc(m_ready, 1)

            with act.Fori(1, BODIES + 1) as r:
                for u in range(U):
                    act.wait_ge(dstb_loaded[u], r * 16 + BODIES * 16)
                    hot_pairs(r, u)
                    act.wait_ge(dist_done, act.snap(pair) - 1)
                    act.sem_inc(dstb_used, 1)
                    act.wait_ge(delta_ready, group1(r, u))
                    nc.scalar.activation(msg[u % 2][:, :, DIM:AW], delta[:, :].rearrange("p (t h) -> p t h", h=HEADS),
                                         ACT.Exp, scale=SCALE).then_inc(exp_ready, 1)
                    nc.scalar.activation(group_weights(group0(r, u)), delta[:, :], ACT.Exp, scale=SCALE).then_inc(exp_ready, 1)

            with act.Fori(1, K_ITERS) as it:
                with act.Fori(1, BODIES + 1) as r:
                    for u in range(U):
                        act.wait_ge(gathered[u], it * (BODIES * 16 * TILES) + r * (16 * TILES))
                        act.wait_ge(msg_ready, it * G + group1(r, u) + U)
                        next_indices(r, u)

        @block.vector
        def _(dve):
            step = [0]

            def then_wait(ins):
                step[0] += 1
                ins.then_inc(dve_step, 1)
                dve.wait_ge(dve_step, step[0])

            dve.wait_ge(iotas_ready, 8)
            nc.vector.tensor_copy(iota_f[:, :], iota_i[:, :])
            nc.vector.tensor_scalar(neg_node[:, :], node_i[:, :], -1.0, None, ALU.mult)
            then_wait(nc.vector.tensor_copy(part_f[:, :], psub_i[:, :]))
            nc.vector.tensor_scalar(base_f[:, :], node_i[:, :], part_f[:, 0:1], None, ALU.subtract)
            then_wait(nc.vector.tensor_scalar(ident[:, :], iota_f[:, :], part_f[:, 0:1], None, ALU.is_equal))
            nc.vector.tensor_scalar(neg_ident[:, :], ident[:, :], -BIG, None, ALU.mult)
            for h in range(HEADS):
                rows = slice(SUB * h, SUB * (h + 1))
                nc.vector.tensor_copy(place[rows, h, 3 * SUB:4 * SUB], ident[rows, rows])
            nc.vector.tensor_scalar(head_i[:, :], iota_i[0:HEADS, :], 5, None, ALU.arith_shift_right)
            then_wait(nc.vector.tensor_scalar(psub_i[:, :], psub_i[:, :], SUB - 1, None, ALU.bitwise_and))
            nc.vector.tensor_scalar(head_rows[:, :], head_i[:, :], part_f[0:HEADS, 0:1], None, ALU.is_equal)
            then_wait(nc.vector.tensor_copy(psub_f[:, :], psub_i[:, :]))
            then_wait(nc.vector.tensor_scalar(neg_sub[:, :], sub_i[:, :], psub_f[:, 0:1], -1.0, ALU.add, ALU.mult))
            dve.sem_inc(consts_ready, 1)

            dve.wait_ge(minmax_loaded, 16)
            for n, op in enumerate((ALU.min, ALU.max, ALU.min)):
                nc.vector.tensor_reduce(range_i[:, :, n:n + 1], minmax_i, AX.X, op)
            then_wait(nc.vector.tensor_reduce(range_i[:, :, 3:4], minmax_i, AX.X, ALU.max))
            nc.vector.tensor_scalar(range_i[:, :, 0:2], range_i[:, :, 0:2], 7, None, ALU.arith_shift_right)
            then_wait(nc.vector.tensor_scalar(range_i[:, :, 2:4], range_i[:, :, 2:4], 5, None, ALU.arith_shift_right))
            nc.vector.tensor_scalar(range_i[:, :, 1:2], range_i[:, :, 1:2], 1.0, None, ALU.add)
            then_wait(nc.vector.tensor_scalar(range_i[:, :, 3:4], range_i[:, :, 3:4], 1.0, None, ALU.add))
            dve.sem_inc(ranges_ready, 1)

            dve.wait_ge(idx_loaded, 32)
            nc.vector.tensor_copy(dst_f[:, :], dst_i)
            nc.vector.tensor_scalar(src_lo, src_i, P - 1, None, ALU.bitwise_and)
            then_wait(nc.vector.tensor_scalar(src_i, src_i, 7, None, ALU.arith_shift_right))
            then_wait(nc.vector.scalar_tensor_tensor(out=idx_all[:, :], in0=src_lo, scalar=float(NB), in1=src_i,
                                                     op0=ALU.mult, op1=ALU.add))
            dve.sem_inc(idx_ready, 1)

            def over_dim(col):
                return col.unsqueeze(2).broadcast_to([P, NB, DIM])

            dve.wait_ge(x_loaded, 16)
            then_wait(nc.vector.tensor_reduce(ln_sum[:, :], x_v, AX.X, ALU.add))
            then_wait(nc.vector.tensor_scalar(ln_sum[:, :], ln_sum[:, :], 1.0 / DIM, None, ALU.mult))
            nc.vector.tensor_tensor(av, x_v, over_dim(ln_sum[:, :]), ALU.subtract).then_inc(centred, 1)
            dve.wait_ge(squared, 1)
            nc.vector.tensor_reduce(ln_sum[:, :], h_sq.rearrange("p (b d) -> p b d", d=DIM), AX.X, ALU.add).then_inc(var_ready, 1)
            dve.wait_ge(std_ready, 1)
            then_wait(nc.vector.reciprocal(ln_r[:, :], ln_sum[:, :]))
            then_wait(nc.vector.scalar_tensor_tensor(out=h_v, in0=av, scalar=0.0, in1=over_dim(ln_r[:, :]), op0=ALU.max, op1=ALU.mult))
            dve.sem_inc(h_ready, 1)
            nc.vector.tensor_tensor(x_v, x_v, h_v, ALU.add).then_inc(xh_ready, 1)

            with dve.Fori(0, NB // 2) as j:
                dve.wait_ge(h_turned, j + 1)
                nc.vector.tensor_copy(h_t[:, :], ps_a[:, 0:P]).then_inc(h_t_ready, 1)
                dve.wait_ge(qkv_done, j + 1)
                nc.vector.tensor_scalar(q_sb[:, bass.ds(j * 2, 2), :], ps_w[:, :, 0:DIM], 1.0, None, ALU.mult)
                nc.vector.tensor_scalar(av[:, bass.ds(j * 2, 2), :], ps_w[:, :, 2 * DIM:3 * DIM], ALPHA, None, ALU.mult)
                nc.vector.tensor_copy(kv_sb[:, bass.ds(j * 2, 2), :], ps_w[:, :, DIM:3 * DIM]).then_inc(kv_kept, 1)

            dve.wait_ge(ranges_loaded, 16)
            dve.wait_ge(xh_stored, 16)
            dve.sem_inc(gmax_done, 2)
            dve.sem_inc(msg_ready, U)
            maximum = counter(dve, "dve_maximum")

            def p1_logits(r, u):
                g1 = group1(r, u)
                dve.wait_ge(ke_done, g1 + U)
                dve.wait_ge(q_ready, g1)
                nc.vector.tensor_tensor(prod[:, :], ps_a[:, 0:TILES * DIM], q_edge[:, :], ALU.mult).then_inc(prod_done, 1)
                dve.wait_ge(prod_done, g1)
                nc.vector.tensor_reduce(lg[:, :], prod[:, :].rearrange("p (g d) -> p g d", d=HD), AX.X, ALU.add).then_inc(lg_ready, 1)
                dve.wait_ge(lg_ready, g1)
                nc.vector.tensor_scalar(group_weights(group0(r, u)), lg[:, :], 1.0, None, ALU.mult).then_inc(lg_kept, 1)

            def p1_maxima(r, u):
                lo, hi = load_range(dve, r, u, SUBS)
                with dve.Fori(lo, hi) as c:
                    n = dve.snap(maximum)
                    dve.wait_ge(max_psum, n + 2)
                    dve.reg_add(maximum, maximum, 1)
                    nc.vector.tensor_reduce(gmax[:, bass.ds(n % 2, 1)], ps_b[:, bass.ds(n % 2, 1), :], AX.X, ALU.max).then_inc(gmax_done, 1)
                    dve.wait_ge(gmax_done, n + 2)
                    nc.vector.tensor_tensor(m_sub[:, bass.ds(c, 1)], m_sub[:, bass.ds(c, 1)], gmax[:, bass.ds(n % 2, 1)], ALU.max).then_inc(m_sub_ready, 1)

            p1_logits(1, 0)
            with dve.Fori(1, BODIES) as r:
                for u in range(U):
                    p1_maxima(r, u)
                    p1_logits(*((r, u + 1) if u + 1 < U else (r + 1, 0)))
            for u in range(U):
                p1_maxima(BODIES, u)
                if u + 1 < U:
                    p1_logits(BODIES, u + 1)
            nc.vector.drain().then_inc(m_sub_done, 1)

            add = counter(dve, "dve_add")

            def aggregate(r, u, width):
                lo, hi = load_range(dve, r, u, BLOCKS)
                with dve.Fori(lo, hi) as b:
                    n = dve.snap(add)
                    dve.reg_add(add, add, 1)
                    nc.vector.scalar_tensor_tensor(out=hot_en[:, :, :], in0=iota_f[:, :].unsqueeze(1).broadcast_to([P, TILES, P]),
                                                   scalar=base_f[:, bass.ds(b, 1)],
                                                   in1=dst_f[:, bass.ds(group0(r, u) * TILES, TILES)].unsqueeze(2).broadcast_to([P, TILES, P]),
                                                   op0=ALU.add, op1=ALU.is_equal).then_inc(hot_en_ready, 1)
                    dve.wait_ge(agg_psum, n)
                    to = agg[:, bass.ds(b, 1), 0:width].rearrange("p a d -> p (a d)")
                    nc.vector.tensor_tensor(to, to, ps_t[:, 0:width], ALU.add).then_inc(added, 1)

            dve.wait_ge(agg_zeroed, 1)
            with dve.Fori(1, BODIES + 1) as r:
                for u in range(U):
                    g1 = group1(r, u)
                    dve.wait_ge(me_done, g1)
                    nc.vector.tensor_tensor(delta[:, :], group_weights(g1 - 1), ps_q[:, 0:EH], ALU.subtract).then_inc(delta_ready, 1)
                    dve.wait_ge(exp_ready, g1 * 2)
                    dve.wait_ge(vsrc_loaded[u], r * 16)
                    nc.vector.tensor_tensor(
                        msg[u % 2][:, :, 0:DIM].rearrange("p t (h d) -> p t h d", d=HD),
                        z_slot[u].rearrange("p t (h d) -> p t h d", d=HD),
                        msg[u % 2][:, :, DIM:AW].unsqueeze(3).broadcast_to([P, TILES, HEADS, HD]), ALU.mult).then_inc(msg_ready, 1)
                    aggregate(r, u, AW)

            dve.wait_ge(added, dve.snap(add) - 1)
            nc.vector.tensor_scalar(r_den[:, :, :], agg[:, :, DIM:AW], 1e-16, None, ALU.add).then_inc(r_den_step, 1)
            dve.wait_ge(r_den_step, 1)
            nc.vector.reciprocal(r_den[:, :, :], r_den[:, :, :]).then_inc(r_den_step, 1)
            dve.wait_ge(r_den_step, 2)
            nc.vector.tensor_scalar(r_den[:, :, :], r_den[:, :, :], 1.0 - ALPHA, None, ALU.mult).then_inc(r_den_step, 1)
            dve.wait_ge(r_den_step, 3)

            def new_z(it):
                nc.vector.tensor_tensor(r_h[:, :].rearrange("p (b h d) -> p b h d", h=HEADS, d=HD),
                                        agg[:, :, 0:DIM].rearrange("p b (h d) -> p b h d", d=HD),
                                        r_den[:, :, :].unsqueeze(3).broadcast_to([P, NB, HEADS, HD]), ALU.mult).then_inc(z_scaled, 1)
                dve.wait_ge(z_scaled, it)
                nc.vector.tensor_tensor(r_h[:, :], r_h[:, :], r_v[:, :], ALU.add).then_inc(z_ready, 1)

            new_z(1)
            zeroed = counter(dve, "dve_zeroed", 2)
            with dve.Fori(1, K_ITERS) as it:
                wait_next(dve, agg_zeroed, zeroed)
                with dve.Fori(1, BODIES + 1) as r:
                    for u in range(U):
                        dve.wait_ge(gathered[u], it * (BODIES * 16 * TILES) + r * (16 * TILES))
                        nc.vector.tensor_tensor(
                            msg[u % 2][:, :, 0:DIM].rearrange("p t (h d) -> p t h d", d=HD),
                            z_slot[u].rearrange("p t (h d) -> p t h d", d=HD),
                            group_weights(group0(r, u)).rearrange("p (t h) -> p t h", h=HEADS)
                            .unsqueeze(3).broadcast_to([P, TILES, HEADS, HD]), ALU.mult).then_inc(msg_ready, 1)
                        aggregate(r, u, DIM)
                dve.wait_ge(added, dve.snap(add) - 1)
                dve.wait_ge(z_stored, it * 16)
                new_z(it + 1)
            dve.wait_ge(xh_loaded, 16)
            dve.wait_ge(z_ready, K_ITERS)
            nc.vector.scalar_tensor_tensor(out=r_h[:, :], in0=r_h[:, :], scalar=0.0, in1=r_q[:, :],
                                           op0=ALU.max, op1=ALU.add).then_inc(out_ready, 1)

        @block.tensor
        def _(pe):
            pe.wait_ge(w_loaded, 16 * 7)
            pe.wait_ge(consts_ready, 1)
            with pe.Fori(0, NB // 2) as j:
                pe.wait_ge(h_staged, j + 1)
                nc.tensor.transpose(ps_a[:, 0:P], h_stage[:, :], ident[:, :]).then_inc(h_turned, 1)
                pe.wait_ge(h_t_ready, j + 1)
                for half in range(2):
                    rows = slice(half * DIM, (half + 1) * DIM)
                    last = nc.tensor.matmul(ps_w[:, half, 0:3 * DIM], h_t[rows, :], w_qkv[rows, :], start=True, stop=True)
                last.then_inc(qkv_done, 1)

            pe.wait_ge(ranges_loaded, 16)
            pe.wait_ge(kv_kept, NB // 2)
            pe.sem_inc(ke_done, U)
            pe.sem_inc(hot_used, 1)
            pe.sem_inc(max_psum, 2)
            pair = counter(pe, "pe_pair")
            submask = counter(pe, "pe_submask")
            scatter = counter(pe, "pe_scatter")
            message = counter(pe, "pe_message", U + 1)

            def by_edge(r, u, width, rhs, done):
                cols = TILES * width
                nc.tensor.matmul(ps_q[:, 0:cols], zero_bf[:, 0:P], zero_bf[:, 0:cols], start=True, stop=False)
                lo, hi = load_range(pe, r, u, BLOCKS)
                with pe.Fori(lo, hi) as b:
                    pe.wait_ge(hot_ready, pe.snap(pair))
                    pe.reg_add(pair, pair, 1)
                    for t in range(TILES):
                        last = nc.tensor.matmul(ps_q[:, t * width:(t + 1) * width], hot_ne[:, t * P:(t + 1) * P], rhs(b),
                                                start=False, stop=False)
                    last.then_inc(hot_used, 1)
                nc.tensor.matmul(ps_q[:, 0:cols], zero_bf[:, 0:P], zero_bf[:, 0:cols], start=False, stop=True).then_inc(done, 1)

            def p1_ke(r, u):
                pe.wait_ge(ea_loaded[u], r * 16)
                pe.wait_ge(gathered[u], r * (16 * TILES))
                for t in range(TILES):
                    to = ps_a[:, t * DIM:(t + 1) * DIM]
                    nc.tensor.matmul(to, ea_slot[u][:, t * P:(t + 1) * P], w_e[:, :], start=True, stop=False)
                    last = nc.tensor.matmul(to, ident[:, :], kv_slot[u][:, t, 0:DIM], start=False, stop=True)
                last.then_inc(ke_done, 1)

            def p1_q(r, u):
                by_edge(r, u, DIM, lambda b: q_sb[:, bass.ds(b, 1), :].rearrange("p a d -> p (a d)"), q_done)

            def p1_turn(r, u):
                pe.wait_ge(lg_ready, group1(r, u))
                for t in range(TILES):
                    last = nc.tensor.transpose(ps_t[0:HEADS, t * P:(t + 1) * P], lg[:, t * HEADS:(t + 1) * HEADS], ident[:, :])
                last.then_inc(lgt_done, 1)

            def p1_spread(r, u):
                pe.wait_ge(lgt_ready, group1(r, u))
                lo, hi = load_range(pe, r, u, SUBS)
                with pe.Fori(lo, hi) as c:
                    n = pe.snap(submask)
                    pe.wait_ge(gmax_done, n)
                    pe.wait_ge(mask_ready, n)
                    pe.reg_add(submask, submask, 1)
                    to = ps_b[:, bass.ds(n % 2, 1), :].rearrange("p a e -> p (a e)")
                    nc.tensor.matmul(to, head_rows[:, :], lg_t[:, :], start=True, stop=False)
                    nc.tensor.matmul(to, neg_ident[:, :], mask[:, bass.ds(n % 2, 1), :].rearrange("p a e -> p (a e)"),
                                     start=False, stop=True).then_inc(max_psum, 1)

            p1_ke(1, 0)
            p1_q(1, 0)
            with pe.Fori(1, BODIES) as r:
                for u in range(U):
                    nxt = (r, u + 1) if u + 1 < U else (r + 1, 0)
                    p1_turn(r, u)
                    p1_ke(*nxt)
                    p1_q(*nxt)
                    p1_spread(r, u)
            for u in range(U):
                p1_turn(BODIES, u)
                if u + 1 < U:
                    p1_ke(BODIES, u + 1)
                    p1_q(BODIES, u + 1)
                p1_spread(BODIES, u)

            pe.wait_ge(m_sub_done, 1)
            subs = m_sub[:, :].rearrange("p (b c) -> p c b", c=P // SUB)
            for h in range(HEADS):
                for c in range(P // SUB):
                    last = nc.tensor.matmul(ps_w[:, 0, h * NB:(h + 1) * NB], place[:, h, (3 - c) * SUB:(3 - c) * SUB + P], subs[:, c, :],
                                            start=c == 0, stop=c == P // SUB - 1)
            last.then_inc(m_moved, 1)

            def scatter_group(r, u, width):
                lo, hi = load_range(pe, r, u, BLOCKS)
                with pe.Fori(lo, hi) as b:
                    pe.wait_ge(hot_en_ready, pe.snap(scatter))
                    pe.reg_add(scatter, scatter, 1)
                    for t in range(TILES):
                        last = nc.tensor.matmul(ps_t[:, 0:width], hot_en[:, t, :], msg[u % 2][:, t, 0:width],
                                                start=t == 0, stop=t == TILES - 1)
                    last.then_inc(agg_psum, 1)

            pe.wait_ge(m_ready, 1)
            with pe.Fori(1, BODIES + 1) as r:
                for u in range(U):
                    by_edge(r, u, HEADS, lambda b: m_node[:, bass.ds(b, 1), :].rearrange("p a h -> p (a h)"), me_done)
                    wait_next(pe, msg_ready, message)
                    scatter_group(r, u, AW)

            with pe.Fori(1, K_ITERS) as it:
                with pe.Fori(1, BODIES + 1) as r:
                    for u in range(U):
                        wait_next(pe, msg_ready, message)
                        scatter_group(r, u, DIM)


def kernel(x, src, dst, edge_attr_64, L0_gnn_Wq, L0_gnn_Wk, L0_gnn_Wv, L0_gnn_We):
    import concourse.bacc as bacc
    from concourse.bass_utils import run_bass_kernel_spmd

    def pad(a, rows, value=0):
        a = np.asarray(a)
        out = np.full((rows,) + a.shape[1:], value, a.dtype)
        out[:a.shape[0]] = a
        return out

    x_l = pad(x, NB * P).reshape(NB, P, DIM).transpose(1, 0, 2).reshape(P, NB * DIM)
    src_p, dst_p = pad(src, NT * P), pad(dst, NT * P, PAD_NODE)
    src_l = src_p.reshape(NT, P).T
    ea_t = pad(edge_attr_64, NT * P).reshape(G, GE, DIM).transpose(0, 2, 1)
    arrays = {
        "x": x_l,
        "src": np.concatenate([src_l, src_l[:, :U * TILES]], axis=1),
        "dst": dst_p.reshape(NT, P).T,
        "dst_rows": dst_p.reshape(G, GE),
        "dst_minmax": dst_p.reshape(BODIES, U, GE),
        "ea_t": ea_t,
        "wq": np.asarray(L0_gnn_Wq), "wk": np.asarray(L0_gnn_Wk), "wv": np.asarray(L0_gnn_Wv), "we": np.asarray(L0_gnn_We),
    }
    arrays = {f"in_{k}": np.ascontiguousarray(v) for k, v in arrays.items()}
    nc = bacc.Bacc("TRN2", target_bir_lowering=False, num_devices=1)
    aps = [nc.dram_tensor(k, v.shape, mybir.dt.from_np(v.dtype), kind="ExternalInput").ap() for k, v in arrays.items()]
    out = nc.dram_tensor("out_0", (P, NB * DIM), mybir.dt.float32, kind="ExternalOutput").ap()
    build_gnn(nc, *aps, out)
    res = run_bass_kernel_spmd(nc, [arrays], core_ids=[0])
    got = np.asarray(res.results[0]["out_0"]).reshape(P, NB, DIM).transpose(1, 0, 2).reshape(NB * P, DIM)
    return got[:N_NODES]
```

```python
import numpy as np
import concourse.bass as bass
from concourse import mybir
from contextlib import ExitStack

P = 128
N_NODES = 12500
N_EDGES = 200000
DIM = 64
HEADS = 4
HD = DIM // HEADS
K_ITERS = 8
ALPHA = 0.1
LN_EPS = 1e-05
NB = -(-N_NODES // P)
PAD_NODE = NB * P - 1
TILES = 4
GE = TILES * P
U = 4
BODIES = -(-N_EDGES // (GE * U))
G = BODIES * U
NT = G * TILES
SUB = 32
NSB = NB * P // SUB
AW = DIM + HEADS
BIG = 2.0 ** 100
M_INIT = -(2.0 ** 120)
SCALE = 1.0 / HD ** 0.5
PARTS = 3
LROWS = PARTS * HEADS
SROWS = 2 * SUB + LROWS
KV_CHUNK = 7
KV_STORES = NB // 2 // KV_CHUNK
KV_SLOTS = 5


def build_gnn(nc, x, src, dst, dst_rows, ea_t, wq, wk, wv, we, out):
    fp32, bf16, i32, i16 = mybir.dt.float32, mybir.dt.bfloat16, mybir.dt.int32, mybir.dt.int16
    ALU, ACT, AX = mybir.AluOpType, mybir.ActivationFunctionType, mybir.AxisListType

    with ExitStack() as ctx:
        def sb(name, shape, dt=fp32):
            return ctx.enter_context(nc.sbuf_tensor(name, shape, dt))

        def pb(name, shape, dt=fp32):
            return ctx.enter_context(nc.psum_tensor(name, shape, dt))

        def sem(name):
            return ctx.enter_context(nc.semaphore(name))

        def sems(name, n):
            return [sem(f"{name}{i}") for i in range(n)]

        kv_table = nc.dram_tensor("kv_table", [P * NB, 2 * DIM], fp32, kind="Internal").ap()
        z_table = nc.dram_tensor("z_table", [P * NB, DIM], fp32, kind="Internal").ap()
        vsrc = nc.dram_tensor("vsrc", [G, P, TILES * DIM], fp32, kind="Internal").ap()
        xh_dram = nc.dram_tensor("xh_dram", [P, NB * DIM], fp32, kind="Internal").ap()
        dst16 = nc.dram_tensor("dst16", [G, GE], i16, kind="Internal").ap()
        range_dram = nc.dram_tensor("range_dram", [BODIES, U * 4], i32, kind="Internal").ap()

        r_x = sb("r_x", [P, NB * DIM])
        r_h = sb("r_h", [P, NB * DIM])
        r_q = sb("r_q", [P, NB * DIM * PARTS // 2])
        r_v = sb("r_v", [P, NB * DIM])
        r_kv = sb("r_kv", [P, NB * AW + U * TILES * 2 * DIM + U * GE // 2])
        x_v = r_x[:, :].rearrange("p (b d) -> p b d", d=DIM)
        h_v = r_h[:, :].rearrange("p (b d) -> p b d", d=DIM)
        q_parts = r_q[:, :].bitcast(bf16).rearrange("p (b c d) -> p b c d", c=PARTS, d=DIM)
        av = r_v[:, :].rearrange("p (b d) -> p b d", d=DIM)
        kv_sb = r_kv[:, 0:KV_SLOTS * KV_CHUNK * 4 * DIM].rearrange("p (b d) -> p b d", d=2 * DIM)
        assert NT * HEADS == NB * DIM
        weights = r_x
        agg = r_kv[:, 0:NB * AW].rearrange("p (b d) -> p b d", d=AW)
        ring0 = NB * AW
        gather_ring = [r_kv[:, ring0 + u * TILES * 2 * DIM:ring0 + (u + 1) * TILES * 2 * DIM] for u in range(U)]
        ea0 = ring0 + U * TILES * 2 * DIM
        ea_slot = [r_kv[:, ea0 + u * GE // 2:ea0 + (u + 1) * GE // 2] for u in range(U)]
        kv_slot = [g.rearrange("p (t d) -> p t d", d=2 * DIM) for g in gather_ring]
        z_slot = [g[:, 0:TILES * DIM].rearrange("p (t d) -> p t d", d=DIM) for g in gather_ring]
        raw = r_q[:, :].bitcast(i32)
        dst_i, src_i = raw[:, 0:NT], raw[:, NT:2 * NT + U * TILES]
        src_lo = raw[:, 2 * NT + U * TILES:3 * NT + 2 * U * TILES]
        rows_i = r_h[0:BODIES, 0:U * GE].bitcast(i32)
        rows_16 = r_h[0:BODIES, U * GE:U * GE + U * GE // 2].bitcast(i16)
        h_sq = r_kv[:, 0:NB * DIM]

        idx_all = sb("idx_all", [P, NT + U * TILES], i32)
        dst_f = sb("dst_f", [P, NT])
        w_qkv = sb("w_qkv", [P, 3 * DIM])
        w_e = sb("w_e", [P, P])
        iota_i = sb("iota_i", [P, P], i32)
        iota_f = sb("iota_f", [P, P])
        node_i = sb("node_i", [P, NB], i32)
        base_f = sb("base_f", [P, NB])
        part_f = sb("part_f", [P, 1])
        sub_i = sb("sub_i", [2 * SUB, NSB], i32)
        psub_i = sb("psub_i", [P, 1], i32)
        psub_f = sb("psub_f", [P, 1])
        neg_sub = sb("neg_sub", [2 * SUB, NSB])
        node_f = sb("node_f", [P, NB])
        ident_bf = sb("ident_bf", [P, P], bf16)
        q_rest = sb("q_rest", [P, 2, DIM])
        ident = sb("ident", [P, P])
        spread_w = sb("spread_w", [SROWS, 2, P], bf16)
        col_i = sb("col_i", [SROWS, P], i32)
        col_f = sb("col_f", [SROWS, P])
        row_i = sb("row_i", [P, 1], i32)
        row_f = sb("row_f", [P, 1])
        place = sb("place", [P, HEADS, P + 3 * SUB])
        zero_bf = sb("zero_bf", [1, 2 * P], bf16)
        range_i = sb("range_i", [BODIES, U, 4], i32)
        ranges = sb("ranges", [1, G * 4], i32)
        ln_sum = sb("ln_sum", [P, NB])
        ln_r = sb("ln_r", [P, NB])
        eps_col = sb("eps_col", [P, 1])
        h_stage = sb("h_stage", [P, 2 * DIM])
        h_t = sb("h_t", [P, P])
        idx_slot = [sb(f"idx_slot{u}", [P, TILES], i32) for u in range(U)]
        dstb_slot = [sb(f"dstb_slot{u}", [P, GE], i16) for u in range(U)]
        hot_ne = sb("hot_ne", [P, GE], bf16)
        hot_en = [sb(f"hot_en{u}", [P, TILES, P]) for u in range(2)]
        spread_in = sb("spread_in", [SROWS, GE], bf16)
        ke = sb("ke", [P, TILES * DIM])
        prod = sb("prod", [P, TILES * DIM])
        lg = sb("lg", [P, TILES * HEADS])
        lg_rest = sb("lg_rest", [P, TILES * HEADS])
        lg_parts = [sb(f"lg_parts{u}", [P, TILES, PARTS, HEADS], bf16) for u in range(2)]
        gmax = sb("gmax", [P, 2])
        m_sub = sb("m_sub", [P, NSB + 1])
        m_rest = sb("m_rest", [P, NB, HEADS])
        m_parts = sb("m_parts", [P, NB, PARTS, HEADS], bf16)
        delta = [sb(f"delta{u}", [P, TILES * HEADS]) for u in range(2)]
        msg = [sb(f"msg{u}", [P, TILES, AW]) for u in range(2)]
        r_den = sb("r_den", [P, NB, HEADS])

        ps_e = [pb(f"ps_e{u}", [P, 512]) for u in range(2)]
        ps_q = [pb(f"ps_q{u}", [P, 512]) for u in range(2)]
        ps_t = pb("ps_t", [P, 512])
        ps_b = pb("ps_b", [P, 2, 512])

        x_loaded, w_loaded, idx_loaded, rows_loaded = sem("x_loaded"), sem("w_loaded"), sem("idx_loaded"), sem("rows_loaded")
        ranges_ready, ranges_out, ranges_loaded = sem("ranges_ready"), sem("ranges_out"), sem("ranges_loaded")
        iotas_ready, consts_ready, idx_ready = sem("iotas_ready"), sem("consts_ready"), sem("idx_ready")
        dve_step, rows16_ready, rows16_out, w_e_zero = sem("dve_step"), sem("rows16_ready"), sem("rows16_out"), sem("w_e_zero")
        centred, squared, var_ready, std_ready, h_ready, xh_ready = (sem(n) for n in (
            "centred", "squared", "var_ready", "std_ready", "h_ready", "xh_ready"))
        q_high, q_left, q_mid, q_low, extra_added = (sem(n) for n in ("q_high", "q_left", "q_mid", "q_low", "extra_added"))
        h_staged, h_turned, h_t_ready, qkv_done, kv_kept = (sem(n) for n in (
            "h_staged", "h_turned", "h_t_ready", "qkv_done", "kv_kept"))
        xh_stored, xh_loaded = sem("xh_stored"), sem("xh_loaded")
        kv_stored = sems("kv_stored", KV_STORES)
        idx_in_slot = sem("idx_in_slot")
        gathered, ea_loaded, dstb_loaded = sems("gathered", U), sems("ea_loaded", U), sems("dstb_loaded", U)
        vsrc_stored, vsrc_loaded = sems("vsrc_stored", U), sems("vsrc_loaded", U)
        dstb_used = sem("dstb_used")
        hot_ready, hot_used = sem("hot_ready"), sem("hot_used")
        e_done, ke_ready, prod_done = sem("e_done"), sem("ke_ready"), sem("prod_done")
        lg_ready, lg_high, lg_rest1, lg_mid, lg_split = (sem(n) for n in ("lg_ready", "lg_high", "lg_rest1", "lg_mid", "lg_split"))
        lgt_done, lgt_ready = sem("lgt_done"), sem("lgt_ready")
        mask_ready = sem("mask_ready")
        max_psum, gmax_done = sem("max_psum"), sem("gmax_done")
        m_sub_ready, m_sub_done, m_moved, m_step, m_ready = (sem(n) for n in ("m_sub_ready", "m_sub_done", "m_moved", "m_step", "m_ready"))
        delta_ready, exp_ready = sem("delta_ready"), sem("exp_ready")
        msg_ready = sem("msg_ready")
        hot_en_ready, agg_psum, added = sem("hot_en_ready"), sem("agg_psum"), sem("added")
        extra_ready, extra_psum = sem("extra_ready"), sem("extra_psum")
        r_den_step = sem("r_den_step")
        z_scaled, z_ready, agg_zeroed, z_stored = sem("z_scaled"), sem("z_ready"), sem("agg_zeroed"), sem("z_stored")
        out_ready, out_stored = sem("out_ready"), sem("out_stored")

        SAFE = "the ranges are made on the chip from dst, which are nodes"
        BLOCKS, SUBS = 0, 1
        EH = TILES * HEADS

        def group0(r, u):
            return r * U + (u - U)

        def group1(r, u):
            return r * U + (u - U + 1)

        def load_range(eng, r, u, which):
            _, v = nc.values_load_multi_w_load_instructions(
                ranges[0:1, bass.ds(group0(r, u) * 4 + 2 * which, 2)], engines=[eng.engine], min_val=0,
                max_val=(NSB if which == SUBS else NB) - 1, skip_runtime_bounds_check_because=SAFE)
            return v

        def range_of(r, u, which):
            return ranges[0:1, bass.ds(group0(r, u) * 4 + 2 * which, 2)]

        def slot_registers(eng, name):
            return [eng.alloc_register(f"{name}{u}") for u in range(U)]

        def kept(eng, register, bound):
            return eng.snap(register, min_val=0, max_val=bound - 1)

        def counter(eng, name, start=1):
            c = eng.alloc_register(name)
            eng.reg_mov(c, start)
            return c

        def wait_next(eng, semaphore, c, by=1):
            eng.wait_ge(semaphore, eng.snap(c))
            eng.reg_add(c, c, by)

        def group_weights(g):
            return weights[:, bass.ds(g * EH, EH)]

        block = ctx.enter_context(nc.Block())

        @block.sync
        def _(sp):
            sp.dma_start(rows_i, dst_rows.rearrange("(b u) e -> b (u e)", u=U)).then_inc(rows_loaded, 16)
            sp.dma_start(r_x[:, :], x).then_inc(x_loaded, 16)
            sp.dma_start(dst_i, dst).then_inc(idx_loaded, 16)
            sp.dma_start(src_i, src).then_inc(idx_loaded, 16)
            sp.wait_ge(w_e_zero, 1)
            for half in range(2):
                rows = slice(half * DIM, (half + 1) * DIM)
                for n, w in enumerate((wq, wk, wv)):
                    sp.dma_start(w_qkv[rows, n * DIM:(n + 1) * DIM], w).then_inc(w_loaded, 16)
                sp.dma_start(w_e[rows, rows], we).then_inc(w_loaded, 16)
            sp.wait_ge(rows16_ready, 1)
            sp.dma_start(dst16.rearrange("(b u) e -> b (u e)", u=U), rows_16).then_inc(rows16_out, 16)
            sp.wait_ge(ranges_ready, 1)
            sp.dma_start(range_dram, range_i[:, :, :].rearrange("p u a -> p (u a)")).then_inc(ranges_out, 16)
            sp.wait_ge(ranges_out, 16)
            sp.dma_start(ranges[:, :], range_dram.rearrange("b c -> (b c)").unsqueeze(0)).then_inc(ranges_loaded, 16)
            sp.wait_ge(xh_ready, 1)
            sp.dma_start(xh_dram, r_x[:, :]).then_inc(xh_stored, 16)
            kv_rows = kv_table.rearrange("(p b) d -> p b d", b=NB)
            for c in range(KV_STORES):
                sp.wait_ge(kv_kept, (c + 1) * KV_CHUNK)
                n = 2 * KV_CHUNK
                sp.dma_start(kv_rows[:, c * n:(c + 1) * n, :], kv_sb[:, c % KV_SLOTS * n:(c % KV_SLOTS + 1) * n, :]).then_inc(kv_stored[c], 16)

            for c in range(KV_STORES):
                sp.wait_ge(kv_stored[c], 16)
            sp.wait_ge(rows16_out, 16)
            with sp.Fori(1, BODIES + 1) as r:
                for u in range(U):
                    sp.wait_ge(e_done, group1(r, u))
                    sp.dma_start(ea_slot[u], ea_t[bass.ds(group0(r, u), 1), :, :].rearrange("a d e -> (a d) e")).then_inc(ea_loaded[u], 16)
                    sp.wait_ge(dstb_used, group1(r, u))
                    sp.dma_start(dstb_slot[u][:, :], dst16[bass.ds(group0(r, u), 1), :].broadcast_to([P, GE])).then_inc(dstb_loaded[u], 16)
                for u in range(U):
                    sp.wait_ge(gathered[u], r * (16 * TILES))
                    sp.dma_start(vsrc[bass.ds(group0(r, u), 1), :, :].rearrange("a p (t d) -> (a p) t d", d=DIM),
                                 kv_slot[u][:, :, DIM:2 * DIM]).then_inc(vsrc_stored[u], 16)

            sp.wait_ge(dstb_used, G + U)
            for u in range(U):
                sp.wait_ge(vsrc_stored[u], BODIES * 16)
            sp.wait_ge(ke_ready, G)
            with sp.Fori(1, BODIES + 1) as r:
                for u in range(U):
                    sp.wait_ge(delta_ready, group1(r, u))
                    sp.dma_start(dstb_slot[u][:, :], dst16[bass.ds(group0(r, u), 1), :].broadcast_to([P, GE])).then_inc(dstb_loaded[u], 16)
                    sp.wait_ge(msg_ready, group1(r, u))
                    sp.dma_start(gather_ring[u][:, 0:TILES * DIM], vsrc[bass.ds(group0(r, u), 1), :, :].rearrange("a p e -> (a p) e")).then_inc(vsrc_loaded[u], 16)

            sp.wait_ge(xh_stored, 16)
            sp.wait_ge(m_ready, 1)
            sp.dma_start(r_q[:, 0:NB * DIM], xh_dram).then_inc(xh_loaded, 16)
            z_rows = z_table.rearrange("(p b) d -> p (b d)", b=NB)
            with sp.Fori(1, K_ITERS) as it:
                sp.wait_ge(z_ready, it)
                sp.dma_start(z_rows, r_h[:, :]).then_inc(z_stored, 16)
            sp.wait_ge(out_ready, 1)
            sp.dma_start(out, r_h[:, :]).then_inc(out_stored, 16)
            sp.wait_ge(z_stored, 16 * (K_ITERS - 1))
            sp.wait_ge(out_stored, 16)

        @block.gpsimd
        def _(pool):
            nc.gpsimd.memset(w_e[:, :], 0.0).then_inc(w_e_zero, 1)
            nc.gpsimd.iota(iota_i[:, :], [[1, P]], base=0, channel_multiplier=0).then_inc(iotas_ready, 1)
            nc.gpsimd.iota(node_i[:, :], [[P, NB]], base=0, channel_multiplier=1).then_inc(iotas_ready, 1)
            nc.gpsimd.iota(sub_i[:, :], [[SUB, NSB]], base=0, channel_multiplier=1).then_inc(iotas_ready, 1)
            nc.gpsimd.iota(psub_i[:, :], [[0, 1]], base=0, channel_multiplier=1).then_inc(iotas_ready, 1)
            nc.gpsimd.memset(place[:, :, :], 0.0).then_inc(iotas_ready, 1)
            nc.gpsimd.memset(spread_w[:, :, :], 0.0).then_inc(iotas_ready, 1)
            nc.gpsimd.memset(zero_bf[:, :], 0.0).then_inc(iotas_ready, 1)
            nc.gpsimd.memset(m_sub[:, :], M_INIT).then_inc(iotas_ready, 1)
            nc.gpsimd.memset(eps_col[:, :], LN_EPS).then_inc(iotas_ready, 1)

            for c in range(KV_STORES):
                pool.wait_ge(kv_stored[c], 16)
            group = counter(pool, "pool_group")
            with pool.Fori(1, BODIES + 1):
                for u in range(U):
                    wait_next(pool, idx_in_slot, group)
                    for t in range(TILES):
                        pool.indirect_dma_start(
                            out=kv_slot[u][:, t, :], out_offset=None, in_=kv_table,
                            in_offset=bass.IndirectOffsetOnAxis(ap=idx_slot[u][:, t:t + 1], axis=0)).then_inc(gathered[u], 16)

            nc.gpsimd.memset(agg, 0.0).then_inc(agg_zeroed, 1)

            z_read = counter(pool, "pool_z_read")
            z_in_dram = counter(pool, "pool_z_in_dram", 16)
            with pool.Fori(1, K_ITERS):
                wait_next(pool, z_scaled, z_read)
                nc.gpsimd.memset(agg, 0.0).then_inc(agg_zeroed, 1)
                wait_next(pool, z_stored, z_in_dram, 16)
                with pool.Fori(1, BODIES + 1):
                    for u in range(U):
                        wait_next(pool, idx_in_slot, group)
                        for t in range(TILES):
                            pool.indirect_dma_start(
                                out=z_slot[u][:, t, :], out_offset=None, in_=z_table,
                                in_offset=bass.IndirectOffsetOnAxis(ap=idx_slot[u][:, t:t + 1], axis=0)).then_inc(gathered[u], 16)

        def after(r, u, n):
            return (r, u + n) if u + n < U else (r + 1, u + n - U)

        def pipeline(eng, run):
            ahead = max(d for d, _ in run)
            for g in range(-ahead, 0):
                for d, stage in run:
                    if g + d >= 0:
                        stage(1, g + d)
            with eng.Fori(1, BODIES) as r:
                for u in range(U):
                    for d, stage in run:
                        stage(*after(r, u, d))
            for u in range(U):
                for d, stage in run:
                    if u + d < U:
                        stage(BODIES, u + d)

        @block.scalar
        def _(act):
            act.wait_ge(centred, 1)
            nc.scalar.activation(h_sq, r_v[:, :], ACT.Square).then_inc(squared, 1)
            act.wait_ge(var_ready, 1)
            act.wait_ge(iotas_ready, 9)
            nc.scalar.activation(ln_sum[:, :], ln_sum[:, :], ACT.Sqrt, bias=eps_col[:, 0:1], scale=1.0 / DIM).then_inc(std_ready, 1)
            act.wait_ge(h_ready, 1)
            with act.Fori(0, NB // 2) as j:
                nc.scalar.activation(h_stage[:, :], r_h[:, bass.ds(j * (2 * DIM), 2 * DIM)], ACT.Copy).then_inc(h_staged, 1)
                act.wait_ge(h_turned, j + 1)
            act.wait_ge(idx_ready, 1)
            for u in range(U):
                nc.scalar.activation(idx_slot[u][:, :], idx_all[:, u * TILES:(u + 1) * TILES], ACT.Copy).then_inc(idx_in_slot, 1)
            act.sem_inc(dstb_used, U)

            act.wait_ge(ranges_loaded, 16)
            act.wait_ge(consts_ready, 1)
            act.wait_ge(xh_stored, 16)
            submask = counter(act, "act_submask")
            first_sub, last_sub = slot_registers(act, "act_first_sub"), slot_registers(act, "act_last_sub")

            def next_indices(r, u):
                act.wait_ge(idx_ready, 1)
                nc.scalar.activation(idx_slot[u][:, :], idx_all[:, bass.ds(group0(r + 1, u) * TILES, TILES)], ACT.Copy).then_inc(idx_in_slot, 1)

            def mask(u, c):
                wait_next(act, max_psum, submask)
                nc.scalar.activation(spread_in[0:2 * SUB, :], dstb_slot[u][0:2 * SUB, :], ACT.Abs,
                                     bias=neg_sub[:, bass.ds(c, 1)]).then_inc(mask_ready, 1)

            def p1_first_mask(r, u):
                act.wait_ge(lgt_done, group1(r, u))
                act.wait_ge(max_psum, act.snap(submask))
                nc.scalar.activation(spread_in[2 * SUB:SROWS, :], ps_t[2 * SUB:SROWS, :], ACT.Copy).then_inc(lgt_ready, 1)
                act.reg_load((first_sub[u], last_sub[u]), range_of(r, u, SUBS))
                mask(u, kept(act, first_sub[u], NSB))

            def p1_more_masks(r, u):
                lo, last_in = kept(act, first_sub[u], NSB), kept(act, last_sub[u], NSB)
                with act.If(lo + 1 < last_in):
                    with act.Fori(lo + 2, last_in + 1, 2) as c:
                        mask(u, c)
                act.wait_ge(mask_ready, act.snap(submask) - 1)
                act.sem_inc(dstb_used, 1)

            def p1_split(r, u):
                g1 = group1(r, u)
                act.wait_ge(lg_ready, g1)
                nc.scalar.activation(group_weights(g1 - 1), lg[:, :], ACT.Copy)
                nc.scalar.activation(lg_parts[u % 2][:, :, 0, :], lg[:, :].rearrange("p (t h) -> p t h", h=HEADS), ACT.Copy).then_inc(lg_high, 1)

            def p1_indices(r, u):
                act.wait_ge(gathered[u], r * (16 * TILES))
                act.wait_ge(vsrc_stored[u], r * 16)
                act.wait_ge(ke_ready, group1(r, u))
                next_indices(r, u)

            pipeline(act, [(0, p1_first_mask), (1, p1_split), (0, p1_more_masks), (0, p1_indices)])

            def p2_exp(r, u):
                g1 = group1(r, u)
                act.wait_ge(delta_ready, g1 + U)
                nc.scalar.activation(msg[u % 2][:, :, DIM:AW], delta[u % 2][:, :].rearrange("p (t h) -> p t h", h=HEADS),
                                     ACT.Exp, scale=SCALE).then_inc(exp_ready, 1)
                nc.scalar.activation(group_weights(g1 - 1), delta[u % 2][:, :], ACT.Exp, scale=SCALE).then_inc(exp_ready, 1)

            pipeline(act, [(0, p2_exp)])

            with act.Fori(1, K_ITERS) as it:
                with act.Fori(1, BODIES + 1) as r:
                    for u in range(U):
                        act.wait_ge(gathered[u], it * (BODIES * 16 * TILES) + r * (16 * TILES))
                        act.wait_ge(msg_ready, it * G + group1(r, u) + U)
                        next_indices(r, u)

        @block.vector
        def _(dve):
            step = [0]

            def then_wait(ins):
                step[0] += 1
                ins.then_inc(dve_step, 1)
                dve.wait_ge(dve_step, step[0])

            dve.wait_ge(rows_loaded, 16)
            nc.vector.tensor_copy(rows_16, rows_i).then_inc(rows16_ready, 1)
            by_group = rows_i.rearrange("p (u e) -> p u e", u=U)
            nc.vector.tensor_reduce(range_i[:, :, 0:1], by_group, AX.X, ALU.min)
            then_wait(nc.vector.tensor_reduce(range_i[:, :, 1:2], by_group, AX.X, ALU.max))
            nc.vector.tensor_scalar(range_i[:, :, 2:4], range_i[:, :, 0:2], 5, None, ALU.arith_shift_right)
            then_wait(nc.vector.tensor_scalar(range_i[:, :, 0:2], range_i[:, :, 0:2], 7, None, ALU.arith_shift_right))
            dve.sem_inc(ranges_ready, 1)

            dve.wait_ge(iotas_ready, 9)
            nc.vector.tensor_copy(iota_f[:, :], iota_i[:, :])
            nc.vector.tensor_copy(node_f[:, :], node_i[:, :])
            then_wait(nc.vector.tensor_copy(part_f[:, :], psub_i[:, :]))
            nc.vector.tensor_scalar(base_f[:, :], node_i[:, :], part_f[:, 0:1], None, ALU.subtract)
            then_wait(nc.vector.tensor_scalar(ident[:, :], iota_f[:, :], part_f[:, 0:1], None, ALU.is_equal))
            for h in range(HEADS):
                rows = slice(SUB * h, SUB * (h + 1))
                nc.vector.tensor_copy(place[rows, h, 3 * SUB:4 * SUB], ident[rows, rows])
            nc.vector.tensor_copy(ident_bf[:, :], ident[:, :])
            nc.vector.tensor_scalar(col_i[0:2 * SUB, :], iota_i[0:2 * SUB, :], SUB - 1, None, ALU.bitwise_and)
            nc.vector.tensor_scalar(col_i[2 * SUB:SROWS, :], iota_i[2 * SUB:SROWS, :], 5, None, ALU.arith_shift_right)
            nc.vector.tensor_scalar(row_i[:, :], psub_i[:, :], HEADS - 1, None, ALU.bitwise_and)
            then_wait(nc.vector.tensor_scalar(psub_i[:, :], psub_i[:, :], SUB - 1, None, ALU.bitwise_and))
            nc.vector.tensor_copy(col_f[:, :], col_i[:, :])
            nc.vector.tensor_copy(row_f[:, :], row_i[:, :])
            then_wait(nc.vector.tensor_copy(psub_f[:, :], psub_i[:, :]))
            for n in range(2):
                rows = slice(n * SUB, (n + 1) * SUB)
                nc.vector.tensor_scalar(spread_w[rows, n, :], col_f[rows, :], psub_f[rows, 0:1], -BIG, ALU.is_equal, ALU.mult)
                nc.vector.tensor_scalar(spread_w[2 * SUB:SROWS, n, :], col_f[2 * SUB:SROWS, :], row_f[2 * SUB:SROWS, 0:1], None, ALU.is_equal)
            then_wait(nc.vector.tensor_scalar(neg_sub[:, :], sub_i[:, :], -1.0, None, ALU.mult))
            dve.sem_inc(consts_ready, 1)

            dve.wait_ge(idx_loaded, 32)
            nc.vector.tensor_copy(dst_f[:, :], dst_i)
            nc.vector.tensor_scalar(src_lo, src_i, P - 1, None, ALU.bitwise_and)
            then_wait(nc.vector.tensor_scalar(src_i, src_i, 7, None, ALU.arith_shift_right))
            then_wait(nc.vector.scalar_tensor_tensor(out=idx_all[:, :], in0=src_lo, scalar=float(NB), in1=src_i,
                                                     op0=ALU.mult, op1=ALU.add))
            dve.sem_inc(idx_ready, 1)

            def over_dim(col):
                return col.unsqueeze(2).broadcast_to([P, NB, DIM])

            dve.wait_ge(x_loaded, 16)
            then_wait(nc.vector.tensor_reduce(ln_sum[:, :], x_v, AX.X, ALU.add))
            then_wait(nc.vector.tensor_scalar(ln_sum[:, :], ln_sum[:, :], 1.0 / DIM, None, ALU.mult))
            nc.vector.tensor_tensor(av, x_v, over_dim(ln_sum[:, :]), ALU.subtract).then_inc(centred, 1)
            dve.wait_ge(squared, 1)
            nc.vector.tensor_reduce(ln_sum[:, :], h_sq.rearrange("p (b d) -> p b d", d=DIM), AX.X, ALU.add).then_inc(var_ready, 1)
            dve.wait_ge(std_ready, 1)
            then_wait(nc.vector.reciprocal(ln_r[:, :], ln_sum[:, :]))
            dve.wait_ge(rows16_out, 16)
            then_wait(nc.vector.scalar_tensor_tensor(out=h_v, in0=av, scalar=0.0, in1=over_dim(ln_r[:, :]), op0=ALU.max, op1=ALU.mult))
            dve.sem_inc(h_ready, 1)
            nc.vector.tensor_tensor(x_v, x_v, h_v, ALU.add).then_inc(xh_ready, 1)

            q_step = counter(dve, "dve_q_step")
            for ch in range(KV_STORES):
                if ch >= KV_SLOTS:
                    dve.wait_ge(kv_stored[ch - KV_SLOTS], 16)
                with dve.Fori(ch * KV_CHUNK, (ch + 1) * KV_CHUNK) as j:
                    dve.wait_ge(h_turned, j + 1)
                    nc.vector.tensor_copy(h_t[:, :], ps_e[0][:, 0:P]).then_inc(h_t_ready, 1)
                    dve.wait_ge(qkv_done, j + 1)
                    high = q_parts[:, bass.ds(j * 2, 2), 0, :]
                    nc.vector.tensor_scalar(high, ps_b[:, :, 0:DIM], 1.0, None, ALU.mult).then_inc(q_high, 1)
                    nc.vector.tensor_scalar(av[:, bass.ds(j * 2, 2), :], ps_b[:, :, 2 * DIM:3 * DIM], ALPHA, None, ALU.mult)
                    dve.wait_ge(q_high, dve.snap(q_step))
                    nc.vector.tensor_tensor(q_rest[:, :, :], ps_b[:, :, 0:DIM], high, ALU.subtract).then_inc(q_left, 1)
                    nc.vector.tensor_copy(kv_sb[:, bass.ds(j * 2 - (ch // KV_SLOTS) * (2 * KV_SLOTS * KV_CHUNK), 2), :],
                                          ps_b[:, :, DIM:3 * DIM]).then_inc(kv_kept, 1)
                    dve.wait_ge(q_left, dve.snap(q_step))
                    mid = q_parts[:, bass.ds(j * 2, 2), 1, :]
                    nc.vector.tensor_scalar(mid, q_rest[:, :, :], 1.0, None, ALU.mult).then_inc(q_mid, 1)
                    dve.wait_ge(q_mid, dve.snap(q_step))
                    dve.reg_add(q_step, q_step, 1)
                    nc.vector.tensor_tensor(q_parts[:, bass.ds(j * 2, 2), 2, :], q_rest[:, :, :], mid, ALU.subtract).then_inc(q_low, 1)

            dve.wait_ge(ranges_loaded, 16)
            dve.wait_ge(q_low, NB // 2)
            dve.sem_inc(gmax_done, 1)
            dve.sem_inc(m_sub_ready, 1)
            dve.sem_inc(msg_ready, U)
            maximum = counter(dve, "dve_maximum")
            pair = counter(dve, "dve_pair")
            due = [counter(dve, f"dve_due{n}") for n in range(2)]

            def hot_pairs(r, u, loads):
                lo, last_in = load_range(dve, r, u, BLOCKS)
                with dve.Fori(lo, last_in + 1) as b:
                    n = dve.snap(pair)
                    dve.wait_ge(dstb_loaded[u], loads)
                    dve.wait_ge(hot_used, n)
                    dve.reg_add(pair, pair, 1)
                    nc.vector.tensor_scalar(hot_ne[:, :], dstb_slot[u][:, :], node_f[:, bass.ds(b, 1)], None, ALU.is_equal).then_inc(hot_ready, 1)
                dve.reg_mov(due[u % 2], dve.snap(pair))

            def p1_hot(r, u):
                hot_pairs(r, u, r * 16)

            def p1_logits(r, u):
                g1 = group1(r, u)
                dve.wait_ge(gathered[u], r * (16 * TILES))
                dve.wait_ge(e_done, g1 + U)
                nc.vector.tensor_tensor(ke[:, :].rearrange("p (t d) -> p t d", d=DIM), ps_e[u % 2][:, 0:TILES * DIM].rearrange("p (t d) -> p t d", d=DIM),
                                        kv_slot[u][:, :, 0:DIM], ALU.add).then_inc(ke_ready, 1)
                dve.wait_ge(hot_used, dve.snap(due[u % 2]))
                dve.wait_ge(ke_ready, g1)
                nc.vector.tensor_tensor(prod[:, :], ke[:, :], ps_q[u % 2][:, 0:TILES * DIM], ALU.mult).then_inc(prod_done, 1)
                dve.wait_ge(prod_done, g1)
                nc.vector.tensor_reduce(lg[:, :], prod[:, :].rearrange("p (g d) -> p g d", d=HD), AX.X, ALU.add).then_inc(lg_ready, 1)

            def p1_parts(r, u):
                g1 = group1(r, u)
                dve.wait_ge(lg_high, g1)
                nc.vector.tensor_tensor(lg_rest[:, :].rearrange("p (t h) -> p t h", h=HEADS), lg[:, :].rearrange("p (t h) -> p t h", h=HEADS),
                                        lg_parts[u % 2][:, :, 0, :], ALU.subtract).then_inc(lg_rest1, 1)
                dve.wait_ge(lg_rest1, g1)
                nc.vector.tensor_copy(lg_parts[u % 2][:, :, 1, :], lg_rest[:, :].rearrange("p (t h) -> p t h", h=HEADS)).then_inc(lg_mid, 1)
                dve.wait_ge(lg_mid, g1)
                nc.vector.tensor_tensor(lg_parts[u % 2][:, :, 2, :], lg_rest[:, :].rearrange("p (t h) -> p t h", h=HEADS),
                                        lg_parts[u % 2][:, :, 1, :], ALU.subtract).then_inc(lg_split, 1)

            def p1_maxima(r, u):
                lo, last_in = load_range(dve, r, u, SUBS)
                with dve.Fori(lo, last_in + 1, 2) as c:
                    dve.reg_add(maximum, maximum, 1)
                    n = dve.snap(maximum)
                    dve.wait_ge(max_psum, n)
                    dve.wait_ge(m_sub_ready, n - 1)
                    nc.vector.tensor_reduce(gmax[:, :], ps_b[:, :, :], AX.X, ALU.max).then_inc(gmax_done, 1)
                    dve.wait_ge(gmax_done, n)
                    nc.vector.tensor_tensor(m_sub[:, bass.ds(c, 2)], m_sub[:, bass.ds(c, 2)], gmax[:, :], ALU.max).then_inc(m_sub_ready, 1)

            pipeline(dve, [(2, p1_hot), (1, p1_logits), (1, p1_parts), (0, p1_maxima)])
            nc.vector.drain().then_inc(m_sub_done, 1)

            dve.wait_ge(m_moved, 1)
            moved = ps_b[:, 0, 0:HEADS * NB].rearrange("p (h b) -> p b h", h=HEADS)
            nc.vector.tensor_copy(m_parts[:, :, 0, :], moved).then_inc(m_step, 1)
            dve.wait_ge(m_step, 1)
            nc.vector.tensor_tensor(m_rest[:, :, :], moved, m_parts[:, :, 0, :], ALU.subtract).then_inc(m_step, 1)
            dve.wait_ge(m_step, 2)
            nc.vector.tensor_copy(m_parts[:, :, 1, :], m_rest[:, :, :]).then_inc(m_step, 1)
            dve.wait_ge(m_step, 3)
            nc.vector.tensor_tensor(m_parts[:, :, 2, :], m_rest[:, :, :], m_parts[:, :, 1, :], ALU.subtract).then_inc(m_ready, 1)

            extra = counter(dve, "dve_extra")
            first_block, last_block = slot_registers(dve, "dve_first_block"), slot_registers(dve, "dve_last_block")

            def build_hot_en(b, r, u):
                return nc.vector.scalar_tensor_tensor(
                    out=hot_en[u % 2][:, :, :], in0=iota_f[:, :].unsqueeze(1).broadcast_to([P, TILES, P]), scalar=base_f[:, bass.ds(b, 1)],
                    in1=dst_f[:, bass.ds(group0(r, u) * TILES, TILES)].unsqueeze(2).broadcast_to([P, TILES, P]),
                    op0=ALU.add, op1=ALU.is_equal)

            def add(b, u, width):
                to = agg[:, bass.ds(b, 1), 0:width].rearrange("p a d -> p (a d)")
                return nc.vector.tensor_tensor(to, to, ps_b[:, u % 2, 0:width], ALU.add)

            def aggregate(r, u, width):
                dve.reg_load((first_block[u], last_block[u]), range_of(r, u, BLOCKS))
                lo, last_in = kept(dve, first_block[u], NB), kept(dve, last_block[u], NB)
                with dve.If(lo < last_in):
                    with dve.Fori(lo, last_in) as b:
                        build_hot_en(b, r, u).then_inc(extra_ready, 1)
                        wait_next(dve, extra_psum, extra)
                        add(b, u, width).then_inc(extra_added, 1)
                        dve.wait_ge(extra_added, dve.snap(extra) - 1)
                build_hot_en(last_in, r, u).then_inc(hot_en_ready, 1)

            def add_last(r, u, g1, width):
                last_in = kept(dve, last_block[u], NB)
                dve.wait_ge(agg_psum, g1)
                dve.wait_ge(added, g1)
                add(last_in, u, width).then_inc(added, 1)

            def p2_hot(r, u):
                hot_pairs(r, u, r * 16 + BODIES * 16)

            def p2_delta(r, u):
                g1 = group1(r, u)
                dve.wait_ge(hot_used, dve.snap(due[u % 2]))
                nc.vector.tensor_tensor(delta[u % 2][:, :], group_weights(g1 - 1), ps_q[u % 2][:, 0:EH], ALU.subtract).then_inc(delta_ready, 1)

            def p2_messages(r, u):
                g1 = group1(r, u)
                dve.wait_ge(exp_ready, g1 * 2)
                dve.wait_ge(vsrc_loaded[u], r * 16)
                nc.vector.tensor_tensor(
                    msg[u % 2][:, :, 0:DIM].rearrange("p t (h d) -> p t h d", d=HD),
                    z_slot[u].rearrange("p t (h d) -> p t h d", d=HD),
                    msg[u % 2][:, :, DIM:AW].unsqueeze(3).broadcast_to([P, TILES, HEADS, HD]), ALU.mult).then_inc(msg_ready, 1)
                aggregate(r, u, AW)

            def p2_add(r, u):
                add_last(r, u, group1(r, u), AW)

            dve.wait_ge(agg_zeroed, 1)
            dve.sem_inc(delta_ready, U)
            dve.sem_inc(added, 1)
            pipeline(dve, [(3, p2_hot), (1, p2_messages), (0, p2_add), (2, p2_delta)])

            dve.wait_ge(added, G + 1)
            nc.vector.tensor_scalar(r_den[:, :, :], agg[:, :, DIM:AW], 1e-16, None, ALU.add).then_inc(r_den_step, 1)
            dve.wait_ge(r_den_step, 1)
            nc.vector.reciprocal(r_den[:, :, :], r_den[:, :, :]).then_inc(r_den_step, 1)
            dve.wait_ge(r_den_step, 2)
            nc.vector.tensor_scalar(r_den[:, :, :], r_den[:, :, :], 1.0 - ALPHA, None, ALU.mult).then_inc(r_den_step, 1)
            dve.wait_ge(r_den_step, 3)

            def new_z(it):
                nc.vector.tensor_tensor(r_h[:, :].rearrange("p (b h d) -> p b h d", h=HEADS, d=HD),
                                        agg[:, :, 0:DIM].rearrange("p b (h d) -> p b h d", d=HD),
                                        r_den[:, :, :].unsqueeze(3).broadcast_to([P, NB, HEADS, HD]), ALU.mult).then_inc(z_scaled, 1)
                dve.wait_ge(z_scaled, it)
                nc.vector.tensor_tensor(r_h[:, :], r_h[:, :], r_v[:, :], ALU.add).then_inc(z_ready, 1)

            new_z(1)
            zeroed = counter(dve, "dve_zeroed", 2)
            with dve.Fori(1, K_ITERS) as it:
                wait_next(dve, agg_zeroed, zeroed)

                def messages(r, u):
                    dve.wait_ge(gathered[u], it * (BODIES * 16 * TILES) + r * (16 * TILES))
                    nc.vector.tensor_tensor(
                        msg[u % 2][:, :, 0:DIM].rearrange("p t (h d) -> p t h d", d=HD),
                        z_slot[u].rearrange("p t (h d) -> p t h d", d=HD),
                        group_weights(group0(r, u)).rearrange("p (t h) -> p t h", h=HEADS)
                        .unsqueeze(3).broadcast_to([P, TILES, HEADS, HD]), ALU.mult).then_inc(msg_ready, 1)
                    aggregate(r, u, DIM)

                def add_group(r, u):
                    add_last(r, u, it * G + group1(r, u), DIM)

                pipeline(dve, [(1, messages), (0, add_group)])
                dve.wait_ge(z_stored, it * 16)
                dve.wait_ge(added, it * G + (G + 1))
                new_z(it + 1)
            dve.wait_ge(xh_loaded, 16)
            dve.wait_ge(z_ready, K_ITERS)
            nc.vector.scalar_tensor_tensor(out=r_h[:, :], in0=r_h[:, :], scalar=0.0, in1=r_q[:, 0:NB * DIM],
                                           op0=ALU.max, op1=ALU.add).then_inc(out_ready, 1)

        @block.tensor
        def _(pe):
            pe.wait_ge(w_loaded, 16 * 8)
            pe.wait_ge(consts_ready, 1)
            with pe.Fori(0, NB // 2) as j:
                pe.wait_ge(h_staged, j + 1)
                nc.tensor.transpose(ps_e[0][:, 0:P], h_stage[:, :], ident[:, :]).then_inc(h_turned, 1)
                pe.wait_ge(h_t_ready, j + 1)
                for half in range(2):
                    rows = slice(half * DIM, (half + 1) * DIM)
                    last = nc.tensor.matmul(ps_b[:, half, 0:3 * DIM], h_t[rows, :], w_qkv[rows, :], start=True, stop=True)
                last.then_inc(qkv_done, 1)

            pe.wait_ge(ranges_loaded, 16)
            pe.wait_ge(kv_kept, NB // 2)
            pe.sem_inc(e_done, U)
            pe.sem_inc(hot_used, 1)
            pe.sem_inc(max_psum, 1)
            pair = counter(pe, "pe_pair")
            submask = counter(pe, "pe_submask")
            group = counter(pe, "pe_group")
            extra = counter(pe, "pe_extra")

            def by_edge(r, u, width, parts):
                cols = TILES * width
                nc.tensor.matmul(ps_q[u % 2][:, 0:cols], zero_bf[:, 0:P], zero_bf[:, 0:cols], start=True, stop=True)
                lo, last_in = load_range(pe, r, u, BLOCKS)
                with pe.Fori(lo, last_in + 1) as b:
                    wait_next(pe, hot_ready, pair)
                    for t in range(TILES):
                        for part in range(PARTS):
                            last = nc.tensor.matmul(ps_q[u % 2][:, t * width:(t + 1) * width], hot_ne[:, t * P:(t + 1) * P],
                                                    parts[:, bass.ds(b, 1), part, :].rearrange("p a d -> p (a d)"),
                                                    start=False, stop=True, skip_group_check=True)
                    last.then_inc(hot_used, 1)

            def p1_e(r, u):
                pe.wait_ge(ea_loaded[u], r * 16)
                for j in range(TILES // 2):
                    last = nc.tensor.matmul(ps_e[u % 2][:, j * P:(j + 1) * P], ea_slot[u][:, j * P:(j + 1) * P], w_e[:, :], start=True, stop=True)
                last.then_inc(e_done, 1)

            def p1_q(r, u):
                by_edge(r, u, DIM, q_parts)

            def p1_turn(r, u):
                pe.wait_ge(lg_split, group1(r, u))
                for t in range(TILES):
                    last = nc.tensor.matmul(ps_t[2 * SUB:SROWS, t * P:(t + 1) * P], lg_parts[u % 2][:, t, :, :].rearrange("p c h -> p (c h)"),
                                            ident_bf[:, :], start=True, stop=True)
                last.then_inc(lgt_done, 1)

            def p1_spread(r, u):
                lo, last_in = load_range(pe, r, u, SUBS)
                with pe.Fori(lo, last_in + 1, 2):
                    n = pe.snap(submask)
                    pe.wait_ge(lgt_ready, group1(r, u))
                    pe.wait_ge(gmax_done, n)
                    pe.wait_ge(mask_ready, n)
                    pe.reg_add(submask, submask, 1)
                    for half in range(2):
                        last = nc.tensor.matmul(ps_b[:, half, :], spread_w[:, half, :], spread_in[:, :], start=True, stop=True)
                    last.then_inc(max_psum, 1)

            pipeline(pe, [(0, p1_turn), (2, p1_e), (2, p1_q), (0, p1_spread)])

            pe.wait_ge(m_sub_done, 1)
            subs = m_sub[:, 0:NSB].rearrange("p (b c) -> p c b", c=P // SUB)
            for h in range(HEADS):
                for c in range(P // SUB):
                    last = nc.tensor.matmul(ps_b[:, 0, h * NB:(h + 1) * NB], place[:, h, (3 - c) * SUB:(3 - c) * SUB + P], subs[:, c, :],
                                            start=c == 0, stop=c == P // SUB - 1)
            last.then_inc(m_moved, 1)

            def scatter_block(u, width):
                for t in range(TILES):
                    last = nc.tensor.matmul(ps_b[:, u % 2, 0:width], hot_en[u % 2][:, t, :], msg[u % 2][:, t, 0:width],
                                            start=t == 0, stop=t == TILES - 1)
                return last

            def scatter_group(r, u, width):
                lo, last_in = load_range(pe, r, u, BLOCKS)
                with pe.If(lo < last_in):
                    with pe.Fori(lo, last_in):
                        wait_next(pe, extra_ready, extra)
                        scatter_block(u, width).then_inc(extra_psum, 1)
                wait_next(pe, hot_en_ready, group)
                scatter_block(u, width).then_inc(agg_psum, 1)

            pe.wait_ge(m_ready, 1)
            def p2_max(r, u):
                pe.wait_ge(delta_ready, group1(r, u) - 2 + U)
                by_edge(r, u, HEADS, m_parts)

            pipeline(pe, [(0, lambda r, u: scatter_group(r, u, AW)), (3, p2_max)])

            with pe.Fori(1, K_ITERS):
                pipeline(pe, [(0, lambda r, u: scatter_group(r, u, DIM))])


def kernel(x, src, dst, edge_attr_64, L0_gnn_Wq, L0_gnn_Wk, L0_gnn_Wv, L0_gnn_We):
    import concourse.bacc as bacc
    from concourse.bass_utils import run_bass_kernel_spmd

    def pad(a, rows, value=0):
        a = np.asarray(a)
        out = np.full((rows,) + a.shape[1:], value, a.dtype)
        out[:a.shape[0]] = a
        return out

    x_l = pad(x, NB * P).reshape(NB, P, DIM).transpose(1, 0, 2).reshape(P, NB * DIM)
    src_p, dst_p = pad(src, NT * P), pad(dst, NT * P, PAD_NODE)
    src_l = src_p.reshape(NT, P).T
    ea_t = pad(edge_attr_64, NT * P).reshape(G, TILES // 2, 2, P, DIM).transpose(0, 2, 4, 1, 3).reshape(G, P, GE // 2)
    arrays = {
        "x": x_l,
        "src": np.concatenate([src_l, src_l[:, :U * TILES]], axis=1),
        "dst": dst_p.reshape(NT, P).T,
        "dst_rows": dst_p.reshape(G, GE),
        "ea_t": ea_t,
        "wq": np.asarray(L0_gnn_Wq), "wk": np.asarray(L0_gnn_Wk), "wv": np.asarray(L0_gnn_Wv), "we": np.asarray(L0_gnn_We),
    }
    arrays = {f"in_{k}": np.ascontiguousarray(v) for k, v in arrays.items()}
    nc = bacc.Bacc("TRN2", target_bir_lowering=False, num_devices=1)
    aps = [nc.dram_tensor(k, v.shape, mybir.dt.from_np(v.dtype), kind="ExternalInput").ap() for k, v in arrays.items()]
    out = nc.dram_tensor("out_0", (P, NB * DIM), mybir.dt.float32, kind="ExternalOutput").ap()
    build_gnn(nc, *aps, out)
    res = run_bass_kernel_spmd(nc, [arrays], core_ids=[0])
    got = np.asarray(res.results[0]["out_0"]).reshape(P, NB, DIM).transpose(1, 0, 2).reshape(NB * P, DIM)
    return got[:N_NODES]
```

```python
import numpy as np
import concourse.bass as bass
from concourse import mybir
from contextlib import ExitStack

P = 128
N_NODES = 12500
N_EDGES = 200000
DIM = 64
HEADS = 4
HD = DIM // HEADS
K_ITERS = 8
ALPHA = 0.1
LN_EPS = 1e-05
NB = -(-N_NODES // P)
PAD_NODE = NB * P - 1
TILES = 4
GE = TILES * P
U = 4
BODIES = -(-N_EDGES // (GE * U))
G = BODIES * U
NT = G * TILES
SUB = 32
NSB = NB * P // SUB
AW = DIM + HEADS
BIG = 2.0 ** 100
M_INIT = -(2.0 ** 120)
SCALE = 1.0 / HD ** 0.5
PARTS = 3
LROWS = PARTS * HEADS
SROWS = 2 * SUB + LROWS
KV_CHUNK = 7
KV_STORES = NB // 2 // KV_CHUNK
KV_SLOTS = 5
Z_CHUNKS = 7
CHUNK_BLOCKS = NB // Z_CHUNKS


def build_gnn(nc, x, src, dst, dst_rows, ea_t, wq, wk, wv, we, out):
    fp32, bf16, i32, i16 = mybir.dt.float32, mybir.dt.bfloat16, mybir.dt.int32, mybir.dt.int16
    ALU, ACT, AX = mybir.AluOpType, mybir.ActivationFunctionType, mybir.AxisListType

    with ExitStack() as ctx:
        def sb(name, shape, dt=fp32):
            return ctx.enter_context(nc.sbuf_tensor(name, shape, dt))

        def pb(name, shape, dt=fp32):
            return ctx.enter_context(nc.psum_tensor(name, shape, dt))

        def sem(name):
            return ctx.enter_context(nc.semaphore(name))

        def sems(name, n):
            return [sem(f"{name}{i}") for i in range(n)]

        kv_table = nc.dram_tensor("kv_table", [P * NB, 2 * DIM], fp32, kind="Internal").ap()
        z_table = nc.dram_tensor("z_table", [P * NB, DIM], fp32, kind="Internal").ap()
        vsrc = nc.dram_tensor("vsrc", [G, P, TILES * DIM], fp32, kind="Internal").ap()
        xh_dram = nc.dram_tensor("xh_dram", [P, NB * DIM], fp32, kind="Internal").ap()
        dst16 = nc.dram_tensor("dst16", [G, GE], i16, kind="Internal").ap()
        range_dram = nc.dram_tensor("range_dram", [BODIES, U * 4], i32, kind="Internal").ap()

        r_x = sb("r_x", [P, NB * DIM])
        r_h = sb("r_h", [P, NB * DIM])
        r_q = sb("r_q", [P, NB * DIM * PARTS // 2])
        r_v = sb("r_v", [P, NB * DIM])
        r_kv = sb("r_kv", [P, NB * AW + U * TILES * 2 * DIM + U * GE // 2])
        x_v = r_x[:, :].rearrange("p (b d) -> p b d", d=DIM)
        xh = r_q[:, 0:NB * DIM].rearrange("p (b d) -> p b d", d=DIM)
        h_v = r_h[:, :].rearrange("p (b d) -> p b d", d=DIM)
        q_parts = r_q[:, :].bitcast(bf16).rearrange("p (b c d) -> p b c d", c=PARTS, d=DIM)
        av = r_v[:, :].rearrange("p (b d) -> p b d", d=DIM)
        kv_sb = r_kv[:, 0:KV_SLOTS * KV_CHUNK * 4 * DIM].rearrange("p (b d) -> p b d", d=2 * DIM)
        assert NT * HEADS == NB * DIM
        weights = r_x
        agg = r_kv[:, 0:NB * AW].rearrange("p (b d) -> p b d", d=AW)
        ring0 = NB * AW
        gather_ring = [r_kv[:, ring0 + u * TILES * 2 * DIM:ring0 + (u + 1) * TILES * 2 * DIM] for u in range(U)]
        ea0 = ring0 + U * TILES * 2 * DIM
        ea_slot = [r_kv[:, ea0 + u * GE // 2:ea0 + (u + 1) * GE // 2] for u in range(U)]
        hot_extra = r_kv[:, ea0:ea0 + GE].rearrange("p (t n) -> p t n", n=P)
        kv_slot = [g.rearrange("p (t d) -> p t d", d=2 * DIM) for g in gather_ring]
        z_slot = [g[:, 0:TILES * DIM].rearrange("p (t d) -> p t d", d=DIM) for g in gather_ring]
        raw = r_q[:, :].bitcast(i32)
        dst_i, src_i = raw[:, 0:NT], raw[:, NT:2 * NT + U * TILES]
        src_lo = raw[:, 2 * NT + U * TILES:3 * NT + 2 * U * TILES]
        rows_i = r_h[0:BODIES, 0:U * GE].bitcast(i32)
        rows_16 = r_h[0:BODIES, U * GE:U * GE + U * GE // 2].bitcast(i16)
        h_sq = r_kv[:, 0:NB * DIM]

        idx_all = sb("idx_all", [P, NT + U * TILES], i32)
        dst_f = sb("dst_f", [P, NT])
        w_qkv = sb("w_qkv", [P, 3 * DIM])
        w_e = sb("w_e", [P, P])
        iota_i = sb("iota_i", [P, P], i32)
        iota_f = sb("iota_f", [P, P])
        node_i = sb("node_i", [P, NB], i32)
        base_f = sb("base_f", [P, NB])
        part_f = sb("part_f", [P, 1])
        sub_i = sb("sub_i", [2 * SUB, NSB], i32)
        psub_i = sb("psub_i", [P, 1], i32)
        psub_f = sb("psub_f", [P, 1])
        neg_sub = sb("neg_sub", [2 * SUB, NSB])
        node_f = sb("node_f", [P, NB])
        ident_bf = sb("ident_bf", [P, P], bf16)
        ident = sb("ident", [P, P])
        spread_w = sb("spread_w", [SROWS, 2, P], bf16)
        col_i = sb("col_i", [SROWS, P], i32)
        col_f = sb("col_f", [SROWS, P])
        row_i = sb("row_i", [P, 1], i32)
        row_f = sb("row_f", [P, 1])
        place = sb("place", [P, HEADS, P + 3 * SUB])
        zero_bf = sb("zero_bf", [1, 2 * P], bf16)
        range_i = sb("range_i", [BODIES, U, 4], i32)
        ranges = sb("ranges", [1, G * 4], i32)
        ln_sum = sb("ln_sum", [P, NB])
        ln_r = sb("ln_r", [P, NB])
        eps_col = sb("eps_col", [P, 1])
        h_stage = sb("h_stage", [P, 2 * DIM])
        h_t = sb("h_t", [P, P])
        idx_slot = [sb(f"idx_slot{u}", [P, TILES], i32) for u in range(U)]
        dstb_slot = [sb(f"dstb_slot{u}", [P, GE], i16) for u in range(U)]
        hot_ne = sb("hot_ne", [P, GE], bf16)
        hot_en = [sb(f"hot_en{u}", [P, TILES, P]) for u in range(2)]
        spread_in = sb("spread_in", [SROWS, GE], bf16)
        ke = sb("ke", [P, TILES * DIM])
        prod = sb("prod", [P, TILES * DIM])
        lg = sb("lg", [P, TILES * HEADS])
        lg_rest = sb("lg_rest", [P, TILES * HEADS])
        lg_parts = [sb(f"lg_parts{u}", [P, TILES, PARTS, HEADS], bf16) for u in range(2)]
        gmax = sb("gmax", [P, 2])
        m_sub = sb("m_sub", [P, NSB + 1])
        m_rest = sb("m_rest", [P, NB, HEADS])
        m_parts = sb("m_parts", [P, NB, PARTS, HEADS], bf16)
        delta = [sb(f"delta{u}", [P, TILES * HEADS]) for u in range(2)]
        msg = [sb(f"msg{u}", [P, TILES, AW]) for u in range(2)]
        r_den = sb("r_den", [P, NB, HEADS])

        ps_e = [pb(f"ps_e{u}", [P, 512]) for u in range(2)]
        ps_q2 = pb("ps_q2", [P, 2, 512])
        ps_q = [ps_q2[:, u, :] for u in range(2)]
        ps_t = pb("ps_t", [P, 512])
        ps_b = pb("ps_b", [P, 2, 512])
        ps_qkv = [ps_b, ps_q2]

        x_loaded, w_loaded, idx_loaded, rows_loaded = sem("x_loaded"), sem("w_loaded"), sem("idx_loaded"), sem("rows_loaded")
        ranges_ready, ranges_out, ranges_loaded = sem("ranges_ready"), sem("ranges_out"), sem("ranges_loaded")
        iotas_ready, consts_ready, idx_ready = sem("iotas_ready"), sem("consts_ready"), sem("idx_ready")
        dve_step, rows16_ready, rows16_out, w_e_zero = sem("dve_step"), sem("rows16_ready"), sem("rows16_out"), sem("w_e_zero")
        centred, squared, var_ready, std_ready, h_ready, xh_ready = (sem(n) for n in (
            "centred", "squared", "var_ready", "std_ready", "h_ready", "xh_ready"))
        h_staged, h_turned, h_t_ready, qkv_done, kv_kept = (sem(n) for n in (
            "h_staged", "h_turned", "h_t_ready", "qkv_done", "kv_kept"))
        xh_stored, xh_loaded = sem("xh_stored"), sem("xh_loaded")
        kv_stored = sems("kv_stored", KV_STORES)
        idx_in_slot = sem("idx_in_slot")
        gathered, ea_loaded, dstb_loaded = sems("gathered", U), sems("ea_loaded", U), sems("dstb_loaded", U)
        vsrc_stored, vsrc_loaded = sems("vsrc_stored", U), sems("vsrc_loaded", U)
        dstb_used = sem("dstb_used")
        hot_ready, hot_used = sem("hot_ready"), sem("hot_used")
        e_done, ke_ready, prod_done = sem("e_done"), sem("ke_ready"), sem("prod_done")
        lg_ready, lg_high, lg_rest1, lg_mid, lg_split = (sem(n) for n in ("lg_ready", "lg_high", "lg_rest1", "lg_mid", "lg_split"))
        lg_kept = sem("lg_kept")
        lgt_done, lgt_ready = sem("lgt_done"), sem("lgt_ready")
        mask_ready = sem("mask_ready")
        max_psum, gmax_done = sem("max_psum"), sem("gmax_done")
        m_sub_ready, m_sub_done, m_moved, m_step, m_ready = (sem(n) for n in ("m_sub_ready", "m_sub_done", "m_moved", "m_step", "m_ready"))
        delta_ready, exp_ready = sem("delta_ready"), sem("exp_ready")
        msg_ready = sem("msg_ready")
        hot_en_ready, agg_psum, added = sem("hot_en_ready"), sem("agg_psum"), sem("added")
        extra_ready, extra_psum, extra_added = (sem(n) for n in ("extra_ready", "extra_psum", "extra_added"))
        r_den_step = sem("r_den_step")
        z_ready, agg_zeroed, agg_started, z_stored = sem("z_ready"), sem("agg_zeroed"), sem("agg_started"), sem("z_stored")
        out_ready, out_stored = sem("out_ready"), sem("out_stored")

        SAFE = "the ranges are made on the chip from dst, which are nodes"
        BLOCKS, SUBS = 0, 1
        EH = TILES * HEADS

        def group0(r, u):
            return r * U + (u - U)

        def group1(r, u):
            return r * U + (u - U + 1)

        def load_range(eng, r, u, which):
            _, v = nc.values_load_multi_w_load_instructions(
                ranges[0:1, bass.ds(group0(r, u) * 4 + 2 * which, 2)], engines=[eng.engine], min_val=0,
                max_val=(NSB if which == SUBS else NB) - 1, skip_runtime_bounds_check_because=SAFE)
            return v

        def range_of(r, u, which):
            return ranges[0:1, bass.ds(group0(r, u) * 4 + 2 * which, 2)]

        def z_chunk(c):
            return slice(c * CHUNK_BLOCKS, (c + 1) * CHUNK_BLOCKS)

        def slot_registers(eng, name):
            return [eng.alloc_register(f"{name}{u}") for u in range(U)]

        def kept(eng, register, bound):
            return eng.snap(register, min_val=0, max_val=bound - 1)

        def counter(eng, name, start=1):
            c = eng.alloc_register(name)
            eng.reg_mov(c, start)
            return c

        def wait_next(eng, semaphore, c, by=1):
            eng.wait_ge(semaphore, eng.snap(c))
            eng.reg_add(c, c, by)

        def group_weights(g):
            return weights[:, bass.ds(g * EH, EH)]

        block = ctx.enter_context(nc.Block())

        @block.sync
        def _(sp):
            sp.dma_start(rows_i, dst_rows.rearrange("(b u) e -> b (u e)", u=U)).then_inc(rows_loaded, 16)
            sp.dma_start(r_x[:, :], x).then_inc(x_loaded, 16)
            sp.dma_start(dst_i, dst).then_inc(idx_loaded, 16)
            sp.dma_start(src_i, src).then_inc(idx_loaded, 16)
            sp.wait_ge(w_e_zero, 1)
            for half in range(2):
                rows = slice(half * DIM, (half + 1) * DIM)
                for n, w in enumerate((wq, wk, wv)):
                    sp.dma_start(w_qkv[rows, n * DIM:(n + 1) * DIM], w).then_inc(w_loaded, 16)
                sp.dma_start(w_e[rows, rows], we).then_inc(w_loaded, 16)
            sp.wait_ge(rows16_ready, 1)
            sp.dma_start(dst16.rearrange("(b u) e -> b (u e)", u=U), rows_16).then_inc(rows16_out, 16)
            sp.wait_ge(ranges_ready, 1)
            sp.dma_start(range_dram, range_i[:, :, :].rearrange("p u a -> p (u a)")).then_inc(ranges_out, 16)
            sp.wait_ge(ranges_out, 16)
            sp.dma_start(ranges[:, :], range_dram.rearrange("b c -> (b c)").unsqueeze(0)).then_inc(ranges_loaded, 16)
            sp.wait_ge(xh_ready, 1)
            sp.dma_start(xh_dram, r_x[:, :]).then_inc(xh_stored, 16)
            kv_rows = kv_table.rearrange("(p b) d -> p b d", b=NB)
            for c in range(KV_STORES):
                sp.wait_ge(kv_kept, (c + 1) * KV_CHUNK + 2)
                n = 2 * KV_CHUNK
                sp.dma_start(kv_rows[:, c * n:(c + 1) * n, :], kv_sb[:, c % KV_SLOTS * n:(c % KV_SLOTS + 1) * n, :]).then_inc(kv_stored[c], 16)

            for c in range(KV_STORES):
                sp.wait_ge(kv_stored[c], 16)
            sp.wait_ge(rows16_out, 16)
            with sp.Fori(1, BODIES + 1) as r:
                for u in range(U):
                    sp.wait_ge(e_done, group1(r, u))
                    sp.dma_start(ea_slot[u], ea_t[bass.ds(group0(r, u), 1), :, :].rearrange("a d e -> (a d) e")).then_inc(ea_loaded[u], 16)
                    sp.wait_ge(dstb_used, group1(r, u))
                    sp.dma_start(dstb_slot[u][:, :], dst16[bass.ds(group0(r, u), 1), :].broadcast_to([P, GE])).then_inc(dstb_loaded[u], 16)
                for u in range(U):
                    sp.wait_ge(gathered[u], r * (16 * TILES))
                    sp.dma_start(vsrc[bass.ds(group0(r, u), 1), :, :].rearrange("a p (t d) -> (a p) t d", d=DIM),
                                 kv_slot[u][:, :, DIM:2 * DIM]).then_inc(vsrc_stored[u], 16)

            sp.wait_ge(dstb_used, G + U)
            for u in range(U):
                sp.wait_ge(vsrc_stored[u], BODIES * 16)
            sp.wait_ge(ke_ready, G)
            with sp.Fori(1, BODIES + 1) as r:
                for u in range(U):
                    sp.wait_ge(delta_ready, group1(r, u))
                    sp.dma_start(dstb_slot[u][:, :], dst16[bass.ds(group0(r, u), 1), :].broadcast_to([P, GE])).then_inc(dstb_loaded[u], 16)
                    sp.wait_ge(msg_ready, group1(r, u))
                    sp.dma_start(gather_ring[u][:, 0:TILES * DIM], vsrc[bass.ds(group0(r, u), 1), :, :].rearrange("a p e -> (a p) e")).then_inc(vsrc_loaded[u], 16)

            sp.wait_ge(xh_stored, 16)
            sp.wait_ge(m_ready, 1)
            sp.dma_start(r_q[:, 0:NB * DIM], xh_dram).then_inc(xh_loaded, 16)
            z_rows = z_table.rearrange("(p b) d -> p b d", b=NB)
            out_rows = out.rearrange("p (b d) -> p b d", d=DIM)
            with sp.Fori(1, K_ITERS) as it:
                for c in range(Z_CHUNKS):
                    sp.wait_ge(z_ready, it * Z_CHUNKS + (c + 1 - Z_CHUNKS))
                    sp.dma_start(z_rows[:, z_chunk(c), :], h_v[:, z_chunk(c), :]).then_inc(z_stored, 16)
            for c in range(Z_CHUNKS):
                sp.wait_ge(out_ready, c + 1)
                sp.dma_start(out_rows[:, z_chunk(c), :], h_v[:, z_chunk(c), :]).then_inc(out_stored, 16)
            sp.wait_ge(z_stored, 16 * Z_CHUNKS * (K_ITERS - 1))
            sp.wait_ge(out_stored, 16 * Z_CHUNKS)

        @block.gpsimd
        def _(pool):
            nc.gpsimd.memset(w_e[:, :], 0.0).then_inc(w_e_zero, 1)
            nc.gpsimd.iota(iota_i[:, :], [[1, P]], base=0, channel_multiplier=0).then_inc(iotas_ready, 1)
            nc.gpsimd.iota(node_i[:, :], [[P, NB]], base=0, channel_multiplier=1).then_inc(iotas_ready, 1)
            nc.gpsimd.iota(sub_i[:, :], [[SUB, NSB]], base=0, channel_multiplier=1).then_inc(iotas_ready, 1)
            nc.gpsimd.iota(psub_i[:, :], [[0, 1]], base=0, channel_multiplier=1).then_inc(iotas_ready, 1)
            nc.gpsimd.memset(place[:, :, :], 0.0).then_inc(iotas_ready, 1)
            nc.gpsimd.memset(spread_w[:, :, :], 0.0).then_inc(iotas_ready, 1)
            nc.gpsimd.memset(zero_bf[:, :], 0.0).then_inc(iotas_ready, 1)
            nc.gpsimd.memset(m_sub[:, :], M_INIT).then_inc(iotas_ready, 1)
            nc.gpsimd.memset(eps_col[:, :], LN_EPS).then_inc(iotas_ready, 1)

            for c in range(KV_STORES):
                pool.wait_ge(kv_stored[c], 16)
            group = counter(pool, "pool_group")
            with pool.Fori(1, BODIES + 1):
                for u in range(U):
                    wait_next(pool, idx_in_slot, group)
                    for t in range(TILES):
                        pool.indirect_dma_start(
                            out=kv_slot[u][:, t, :], out_offset=None, in_=kv_table,
                            in_offset=bass.IndirectOffsetOnAxis(ap=idx_slot[u][:, t:t + 1], axis=0)).then_inc(gathered[u], 16)

            nc.gpsimd.memset(agg, 0.0).then_inc(agg_zeroed, 1)

            z_in_dram = counter(pool, "pool_z_in_dram", 16 * Z_CHUNKS)
            with pool.Fori(1, K_ITERS):
                wait_next(pool, z_stored, z_in_dram, 16 * Z_CHUNKS)
                with pool.Fori(1, BODIES + 1):
                    for u in range(U):
                        wait_next(pool, idx_in_slot, group)
                        for t in range(TILES):
                            pool.indirect_dma_start(
                                out=z_slot[u][:, t, :], out_offset=None, in_=z_table,
                                in_offset=bass.IndirectOffsetOnAxis(ap=idx_slot[u][:, t:t + 1], axis=0)).then_inc(gathered[u], 16)

        def by_pair(eng, ch, stage):
            with eng.Fori(0, KV_CHUNK // 2) as i:
                for n in range(2):
                    stage(i * 2 + (ch * KV_CHUNK + n), (ch + n) % 2)
            stage((ch + 1) * KV_CHUNK - 1, ch % 2)

        def after(r, u, n):
            return (r, u + n) if u + n < U else (r + 1, u + n - U)

        def pipeline(eng, run):
            ahead = max(d for d, _ in run)
            for g in range(-ahead, 0):
                for d, stage in run:
                    if g + d >= 0:
                        stage(1, g + d)
            with eng.Fori(1, BODIES) as r:
                for u in range(U):
                    for d, stage in run:
                        stage(*after(r, u, d))
            for u in range(U):
                for d, stage in run:
                    if u + d < U:
                        stage(BODIES, u + d)

        @block.scalar
        def _(act):
            act.wait_ge(centred, 1)
            nc.scalar.activation(h_sq, r_v[:, :], ACT.Square).then_inc(squared, 1)
            act.wait_ge(var_ready, 1)
            act.wait_ge(iotas_ready, 9)
            nc.scalar.activation(ln_sum[:, :], ln_sum[:, :], ACT.Sqrt, bias=eps_col[:, 0:1], scale=1.0 / DIM).then_inc(std_ready, 1)
            act.wait_ge(h_ready, 1)

            def turn_h(j, n):
                nc.scalar.activation(h_stage[:, :], r_h[:, bass.ds(j * (2 * DIM), 2 * DIM)], ACT.Copy).then_inc(h_staged, 1)
                act.wait_ge(h_turned, j + 1)
                nc.scalar.activation(h_t[:, :], ps_e[0][:, 0:P], ACT.Copy).then_inc(h_t_ready, 1)

            for ch in range(KV_STORES):
                by_pair(act, ch, turn_h)
            act.wait_ge(idx_ready, 1)
            for u in range(U):
                nc.scalar.activation(idx_slot[u][:, :], idx_all[:, u * TILES:(u + 1) * TILES], ACT.Copy).then_inc(idx_in_slot, 1)
            act.sem_inc(dstb_used, U)

            act.wait_ge(ranges_loaded, 16)
            act.wait_ge(consts_ready, 1)
            act.wait_ge(xh_stored, 16)
            submask = counter(act, "act_submask")
            first_sub, last_sub = slot_registers(act, "act_first_sub"), slot_registers(act, "act_last_sub")

            def next_indices(r, u):
                act.wait_ge(idx_ready, 1)
                nc.scalar.activation(idx_slot[u][:, :], idx_all[:, bass.ds(group0(r + 1, u) * TILES, TILES)], ACT.Copy).then_inc(idx_in_slot, 1)

            def mask(u, c):
                wait_next(act, max_psum, submask)
                nc.scalar.activation(spread_in[0:2 * SUB, :], dstb_slot[u][0:2 * SUB, :], ACT.Abs,
                                     bias=neg_sub[:, bass.ds(c, 1)]).then_inc(mask_ready, 1)

            def p1_first_mask(r, u):
                act.wait_ge(lgt_done, group1(r, u))
                act.wait_ge(max_psum, act.snap(submask))
                nc.scalar.activation(spread_in[2 * SUB:SROWS, :], ps_t[2 * SUB:SROWS, :], ACT.Copy).then_inc(lgt_ready, 1)
                act.reg_load((first_sub[u], last_sub[u]), range_of(r, u, SUBS))
                mask(u, kept(act, first_sub[u], NSB))

            def p1_more_masks(r, u):
                lo, last_in = kept(act, first_sub[u], NSB), kept(act, last_sub[u], NSB)
                with act.If(lo + 1 < last_in):
                    with act.Fori(lo + 2, last_in + 1, 2) as c:
                        mask(u, c)
                act.wait_ge(mask_ready, act.snap(submask) - 1)
                act.sem_inc(dstb_used, 1)

            def p1_split(r, u):
                g1 = group1(r, u)
                act.wait_ge(lg_ready, g1)
                nc.scalar.activation(lg_parts[u % 2][:, :, 0, :], lg[:, :].rearrange("p (t h) -> p t h", h=HEADS), ACT.Copy).then_inc(lg_high, 1)
                nc.scalar.activation(group_weights(g1 - 1), lg[:, :], ACT.Copy).then_inc(lg_kept, 1)

            def p1_indices(r, u):
                act.wait_ge(gathered[u], r * (16 * TILES))
                act.wait_ge(vsrc_stored[u], r * 16)
                act.wait_ge(ke_ready, group1(r, u))
                next_indices(r, u)

            pipeline(act, [(0, p1_first_mask), (1, p1_split), (0, p1_more_masks), (0, p1_indices)])

            def p2_exp(r, u):
                g1 = group1(r, u)
                act.wait_ge(delta_ready, g1 + U)
                nc.scalar.activation(msg[u % 2][:, :, DIM:AW], delta[u % 2][:, :].rearrange("p (t h) -> p t h", h=HEADS),
                                     ACT.Exp, scale=SCALE).then_inc(exp_ready, 1)
                nc.scalar.activation(group_weights(g1 - 1), delta[u % 2][:, :], ACT.Exp, scale=SCALE).then_inc(exp_ready, 1)

            pipeline(act, [(0, p2_exp)])

            with act.Fori(1, K_ITERS) as it:
                for c in range(Z_CHUNKS):
                    act.wait_ge(z_ready, it * Z_CHUNKS + (c + 1 - Z_CHUNKS))
                    nc.scalar.activation(agg[:, z_chunk(c), 0:DIM], av[:, z_chunk(c), :], ACT.Copy).then_inc(agg_started, 1)
                with act.Fori(1, BODIES + 1) as r:
                    for u in range(U):
                        act.wait_ge(gathered[u], it * (BODIES * 16 * TILES) + r * (16 * TILES))
                        act.wait_ge(msg_ready, it * G + group1(r, u) + U)
                        next_indices(r, u)

        @block.vector
        def _(dve):
            step = [0]

            def then_wait(ins):
                step[0] += 1
                ins.then_inc(dve_step, 1)
                dve.wait_ge(dve_step, step[0])

            dve.wait_ge(rows_loaded, 16)
            nc.vector.tensor_copy(rows_16, rows_i).then_inc(rows16_ready, 1)
            by_group = rows_i.rearrange("p (u e) -> p u e", u=U)
            nc.vector.tensor_reduce(range_i[:, :, 0:1], by_group, AX.X, ALU.min)
            then_wait(nc.vector.tensor_reduce(range_i[:, :, 1:2], by_group, AX.X, ALU.max))
            nc.vector.tensor_scalar(range_i[:, :, 2:4], range_i[:, :, 0:2], 5, None, ALU.arith_shift_right)
            then_wait(nc.vector.tensor_scalar(range_i[:, :, 0:2], range_i[:, :, 0:2], 7, None, ALU.arith_shift_right))
            dve.sem_inc(ranges_ready, 1)

            dve.wait_ge(iotas_ready, 9)
            nc.vector.tensor_copy(iota_f[:, :], iota_i[:, :])
            nc.vector.tensor_copy(node_f[:, :], node_i[:, :])
            then_wait(nc.vector.tensor_copy(part_f[:, :], psub_i[:, :]))
            nc.vector.tensor_scalar(base_f[:, :], node_i[:, :], part_f[:, 0:1], None, ALU.subtract)
            then_wait(nc.vector.tensor_scalar(ident[:, :], iota_f[:, :], part_f[:, 0:1], None, ALU.is_equal))
            for h in range(HEADS):
                rows = slice(SUB * h, SUB * (h + 1))
                nc.vector.tensor_copy(place[rows, h, 3 * SUB:4 * SUB], ident[rows, rows])
            nc.vector.tensor_copy(ident_bf[:, :], ident[:, :])
            nc.vector.tensor_scalar(col_i[0:2 * SUB, :], iota_i[0:2 * SUB, :], SUB - 1, None, ALU.bitwise_and)
            nc.vector.tensor_scalar(col_i[2 * SUB:SROWS, :], iota_i[2 * SUB:SROWS, :], 5, None, ALU.arith_shift_right)
            nc.vector.tensor_scalar(row_i[:, :], psub_i[:, :], HEADS - 1, None, ALU.bitwise_and)
            then_wait(nc.vector.tensor_scalar(psub_i[:, :], psub_i[:, :], SUB - 1, None, ALU.bitwise_and))
            nc.vector.tensor_copy(col_f[:, :], col_i[:, :])
            nc.vector.tensor_copy(row_f[:, :], row_i[:, :])
            then_wait(nc.vector.tensor_copy(psub_f[:, :], psub_i[:, :]))
            for n in range(2):
                rows = slice(n * SUB, (n + 1) * SUB)
                nc.vector.tensor_scalar(spread_w[rows, n, :], col_f[rows, :], psub_f[rows, 0:1], -BIG, ALU.is_equal, ALU.mult)
                nc.vector.tensor_scalar(spread_w[2 * SUB:SROWS, n, :], col_f[2 * SUB:SROWS, :], row_f[2 * SUB:SROWS, 0:1], None, ALU.is_equal)
            then_wait(nc.vector.tensor_scalar(neg_sub[:, :], sub_i[:, :], -1.0, None, ALU.mult))
            dve.sem_inc(consts_ready, 1)

            dve.wait_ge(idx_loaded, 32)
            nc.vector.tensor_copy(dst_f[:, :], dst_i)
            nc.vector.tensor_scalar(src_lo, src_i, P - 1, None, ALU.bitwise_and)
            then_wait(nc.vector.tensor_scalar(src_i, src_i, 7, None, ALU.arith_shift_right))
            then_wait(nc.vector.scalar_tensor_tensor(out=idx_all[:, :], in0=src_lo, scalar=float(NB), in1=src_i,
                                                     op0=ALU.mult, op1=ALU.add))
            dve.sem_inc(idx_ready, 1)

            def over_dim(col):
                return col.unsqueeze(2).broadcast_to([P, NB, DIM])

            dve.wait_ge(x_loaded, 16)
            then_wait(nc.vector.tensor_reduce(ln_sum[:, :], x_v, AX.X, ALU.add))
            then_wait(nc.vector.tensor_scalar(ln_sum[:, :], ln_sum[:, :], 1.0 / DIM, None, ALU.mult))
            nc.vector.tensor_tensor(av, x_v, over_dim(ln_sum[:, :]), ALU.subtract).then_inc(centred, 1)
            dve.wait_ge(squared, 1)
            nc.vector.tensor_reduce(ln_sum[:, :], h_sq.rearrange("p (b d) -> p b d", d=DIM), AX.X, ALU.add).then_inc(var_ready, 1)
            dve.wait_ge(std_ready, 1)
            then_wait(nc.vector.reciprocal(ln_r[:, :], ln_sum[:, :]))
            dve.wait_ge(rows16_out, 16)
            then_wait(nc.vector.scalar_tensor_tensor(out=h_v, in0=av, scalar=0.0, in1=over_dim(ln_r[:, :]), op0=ALU.max, op1=ALU.mult))
            dve.sem_inc(h_ready, 1)
            nc.vector.tensor_tensor(x_v, x_v, h_v, ALU.add).then_inc(xh_ready, 1)

            dve.sem_inc(kv_kept, 2)
            dve.wait_ge(xh_ready, 1)
            for ch in range(KV_STORES):
                if ch >= KV_SLOTS:
                    dve.wait_ge(kv_stored[ch - KV_SLOTS], 16)

                def keep_pair(j, n):
                    dve.wait_ge(qkv_done, j + 1)
                    nc.vector.tensor_copy(h_v[:, bass.ds(j * 2, 2), :], ps_qkv[n][:, :, 0:DIM])
                    nc.vector.tensor_scalar(av[:, bass.ds(j * 2, 2), :], ps_qkv[n][:, :, 2 * DIM:3 * DIM], ALPHA, None, ALU.mult)
                    nc.vector.tensor_copy(kv_sb[:, bass.ds(j * 2 - (ch // KV_SLOTS) * (2 * KV_SLOTS * KV_CHUNK), 2), :],
                                          ps_qkv[n][:, :, DIM:3 * DIM]).then_inc(kv_kept, 1)

                by_pair(dve, ch, keep_pair)
                rows = slice(2 * ch * KV_CHUNK, 2 * (ch + 1) * KV_CHUNK)
                dve.wait_ge(kv_kept, (ch + 1) * KV_CHUNK + 2)
                then_wait(nc.vector.tensor_copy(q_parts[:, rows, 0, :], h_v[:, rows, :]))
                then_wait(nc.vector.tensor_tensor(h_v[:, rows, :], h_v[:, rows, :], q_parts[:, rows, 0, :], ALU.subtract))
                then_wait(nc.vector.tensor_copy(q_parts[:, rows, 1, :], h_v[:, rows, :]))
                then_wait(nc.vector.tensor_tensor(q_parts[:, rows, 2, :], h_v[:, rows, :], q_parts[:, rows, 1, :], ALU.subtract))

            dve.wait_ge(ranges_loaded, 16)
            dve.sem_inc(gmax_done, 1)
            dve.sem_inc(m_sub_ready, 1)
            dve.sem_inc(msg_ready, U)
            dve.sem_inc(lg_kept, 1)
            maximum = counter(dve, "dve_maximum")
            first_sub, last_sub = slot_registers(dve, "dve_first_sub"), slot_registers(dve, "dve_last_sub")
            first_block, last_block = slot_registers(dve, "dve_first_block"), slot_registers(dve, "dve_last_block")
            taken = dve.alloc_register("dve_taken")
            pair = counter(dve, "dve_pair")
            due = [counter(dve, f"dve_due{n}") for n in range(2)]

            def hot_pair(u, b, loads):
                n = dve.snap(pair)
                dve.wait_ge(dstb_loaded[u], loads)
                dve.wait_ge(hot_used, n)
                dve.reg_add(pair, pair, 1)
                nc.vector.tensor_scalar(hot_ne[:, :], dstb_slot[u][:, :], node_f[:, bass.ds(b, 1)], None, ALU.is_equal).then_inc(hot_ready, 1)

            def hot_pairs(u, loads):
                lo, last_in = kept(dve, first_block[u], NB), kept(dve, last_block[u], NB)
                hot_pair(u, lo, loads)
                with dve.If(lo < last_in):
                    with dve.Fori(lo + 1, last_in + 1) as b:
                        hot_pair(u, b, loads)

            def p1_range(r, u):
                dve.reg_load((first_block[u], last_block[u], first_sub[u], last_sub[u]), ranges[0:1, bass.ds(group0(r, u) * 4, 4)])

            def p1_hot(r, u):
                hot_pairs(u, r * 16)
                dve.reg_mov(due[u % 2], dve.snap(pair))

            def p1_logits(r, u):
                g1 = group1(r, u)
                q_pairs = dve.snap(due[u % 2])
                dve.wait_ge(gathered[u], r * (16 * TILES))
                dve.wait_ge(e_done, g1 + U)
                nc.vector.tensor_tensor(ke[:, :].rearrange("p (t d) -> p t d", d=DIM), ps_e[u % 2][:, 0:TILES * DIM].rearrange("p (t d) -> p t d", d=DIM),
                                        kv_slot[u][:, :, 0:DIM], ALU.add).then_inc(ke_ready, 1)
                dve.wait_ge(hot_used, q_pairs)
                dve.wait_ge(ke_ready, g1)
                nc.vector.tensor_tensor(prod[:, :], ke[:, :], ps_q[u % 2][:, 0:TILES * DIM], ALU.mult).then_inc(prod_done, 1)
                dve.wait_ge(prod_done, g1)
                dve.wait_ge(lg_kept, g1)
                nc.vector.tensor_reduce(lg[:, :], prod[:, :].rearrange("p (g d) -> p g d", d=HD), AX.X, ALU.add).then_inc(lg_ready, 1)

            def p1_parts(r, u):
                g1 = group1(r, u)
                dve.wait_ge(lg_high, g1)
                nc.vector.tensor_tensor(lg_rest[:, :].rearrange("p (t h) -> p t h", h=HEADS), lg[:, :].rearrange("p (t h) -> p t h", h=HEADS),
                                        lg_parts[u % 2][:, :, 0, :], ALU.subtract).then_inc(lg_rest1, 1)
                dve.wait_ge(lg_rest1, g1)
                nc.vector.tensor_copy(lg_parts[u % 2][:, :, 1, :], lg_rest[:, :].rearrange("p (t h) -> p t h", h=HEADS)).then_inc(lg_mid, 1)
                dve.wait_ge(lg_mid, g1)
                nc.vector.tensor_tensor(lg_parts[u % 2][:, :, 2, :], lg_rest[:, :].rearrange("p (t h) -> p t h", h=HEADS),
                                        lg_parts[u % 2][:, :, 1, :], ALU.subtract).then_inc(lg_split, 1)

            def take_maxima():
                n = dve.snap(maximum)
                dve.wait_ge(max_psum, n + 1)
                dve.wait_ge(m_sub_ready, n)
                dve.reg_add(maximum, maximum, 1)
                nc.vector.tensor_reduce(gmax[:, :], ps_b[:, :, :], AX.X, ALU.max).then_inc(gmax_done, 1)

            def keep_maxima(c):
                dve.wait_ge(gmax_done, dve.snap(maximum))
                nc.vector.tensor_tensor(m_sub[:, bass.ds(c, 2)], m_sub[:, bass.ds(c, 2)], gmax[:, :], ALU.max).then_inc(m_sub_ready, 1)

            def p1_maxima(r, u):
                lo, last_in = kept(dve, first_sub[u], NSB), kept(dve, last_sub[u], NSB)
                take_maxima()
                dve.reg_mov(taken, lo)
                with dve.If(lo + 1 < last_in):
                    with dve.Fori(lo + 2, last_in + 1, 2) as c:
                        keep_maxima(kept(dve, taken, NSB))
                        take_maxima()
                        dve.reg_mov(taken, c)

            def p1_keep(r, u):
                keep_maxima(kept(dve, taken, NSB))

            pipeline(dve, [(1, p1_logits), (1, p1_parts), (0, p1_maxima), (2, p1_range), (2, p1_hot), (0, p1_keep)])
            nc.vector.drain().then_inc(m_sub_done, 1)

            dve.wait_ge(m_moved, 1)
            moved = ps_b[:, 0, 0:HEADS * NB].rearrange("p (h b) -> p b h", h=HEADS)
            nc.vector.tensor_copy(m_parts[:, :, 0, :], moved).then_inc(m_step, 1)
            dve.wait_ge(m_step, 1)
            nc.vector.tensor_tensor(m_rest[:, :, :], moved, m_parts[:, :, 0, :], ALU.subtract).then_inc(m_step, 1)
            dve.wait_ge(m_step, 2)
            nc.vector.tensor_copy(m_parts[:, :, 1, :], m_rest[:, :, :]).then_inc(m_step, 1)
            dve.wait_ge(m_step, 3)
            nc.vector.tensor_tensor(m_parts[:, :, 2, :], m_rest[:, :, :], m_parts[:, :, 1, :], ALU.subtract).then_inc(m_ready, 1)

            extra = counter(dve, "dve_extra")
            extra_adds = counter(dve, "dve_extra_adds")
            extra_block = counter(dve, "dve_extra_block", 0)

            def build_hot_en(hot, b, r, u):
                return nc.vector.scalar_tensor_tensor(
                    out=hot, in0=iota_f[:, :].unsqueeze(1).broadcast_to([P, TILES, P]), scalar=base_f[:, bass.ds(b, 1)],
                    in1=dst_f[:, bass.ds(group0(r, u) * TILES, TILES)].unsqueeze(2).broadcast_to([P, TILES, P]),
                    op0=ALU.add, op1=ALU.is_equal)

            def add(b, psum, width):
                to = agg[:, bass.ds(b, 1), 0:width].rearrange("p a d -> p (a d)")
                return nc.vector.tensor_tensor(to, to, psum[:, 0:width], ALU.add)

            def add_extra(done, width):
                b, n = kept(dve, extra_block, NB), dve.snap(extra)
                if not (isinstance(done, int) and done == 0):
                    dve.wait_ge(added, done)
                dve.wait_ge(extra_psum, n)
                dve.reg_add(extra, extra, 1)
                add(b, ps_e[0], width).then_inc(extra_added, 1)

            def aggregate(r, u, g1, width):
                lo, last_in = kept(dve, first_block[u], NB), kept(dve, last_block[u], NB)
                with dve.If(lo < last_in):
                    with dve.Fori(lo, last_in) as b:
                        add_extra(g1 - 1, width)
                        build_hot_en(hot_extra, b, r, u).then_inc(extra_ready, 1)
                        dve.reg_mov(extra_block, b)
                        wait_next(dve, extra_added, extra_adds)
                build_hot_en(hot_en[u % 2][:, :, :], last_in, r, u).then_inc(hot_en_ready, 1)

            def add_last(r, u, g1, width):
                last_in = kept(dve, last_block[u], NB)
                dve.wait_ge(agg_psum, g1)
                dve.wait_ge(added, g1)
                add(last_in, ps_b[:, u % 2, :], width).then_inc(added, 1)

            def load_blocks(r, u):
                dve.reg_load((first_block[u], last_block[u]), range_of(r, u, BLOCKS))

            def p2_hot(r, u):
                hot_pairs(u, r * 16 + BODIES * 16)
                dve.reg_mov(due[u % 2], dve.snap(pair))

            def p2_delta(r, u):
                g1 = group1(r, u)
                dve.wait_ge(hot_used, dve.snap(due[u % 2]))
                nc.vector.tensor_tensor(delta[u % 2][:, :], group_weights(g1 - 1), ps_q[u % 2][:, 0:EH], ALU.subtract).then_inc(delta_ready, 1)

            def p2_messages(r, u):
                g1 = group1(r, u)
                dve.wait_ge(exp_ready, g1 * 2)
                dve.wait_ge(vsrc_loaded[u], r * 16)
                nc.vector.tensor_tensor(
                    msg[u % 2][:, :, 0:DIM].rearrange("p t (h d) -> p t h d", d=HD),
                    z_slot[u].rearrange("p t (h d) -> p t h d", d=HD),
                    msg[u % 2][:, :, DIM:AW].unsqueeze(3).broadcast_to([P, TILES, HEADS, HD]), ALU.mult).then_inc(msg_ready, 1)
                aggregate(r, u, g1, AW)

            def p2_add(r, u):
                add_last(r, u, group1(r, u), AW)

            dve.wait_ge(agg_zeroed, 1)
            dve.sem_inc(delta_ready, U)
            dve.sem_inc(added, 1)
            pipeline(dve, [(1, p2_messages), (3, load_blocks), (0, p2_add), (2, p2_delta), (3, p2_hot)])

            add_extra(G + 1, AW)
            wait_next(dve, extra_added, extra_adds)

            dve.wait_ge(added, G + 1)
            by_head = av.rearrange("p b (h d) -> p (b h) d", d=HD)
            nc.vector.tensor_scalar(r_den[:, :, :], agg[:, :, DIM:AW], 1e-16, None, ALU.add).then_inc(r_den_step, 1)
            dve.wait_ge(r_den_step, 1)
            nc.vector.scalar_tensor_tensor(out=by_head, in0=by_head, scalar=1.0 / (1.0 - ALPHA),
                                           in1=r_den[:, :, :].rearrange("p b h -> p (b h)").unsqueeze(2).broadcast_to([P, NB * HEADS, HD]),
                                           op0=ALU.mult, op1=ALU.mult).then_inc(r_den_step, 1)
            dve.wait_ge(r_den_step, 2)
            nc.vector.reciprocal(r_den[:, :, :], r_den[:, :, :]).then_inc(r_den_step, 1)
            nc.vector.tensor_tensor(agg[:, :, 0:DIM], agg[:, :, 0:DIM], av, ALU.add).then_inc(r_den_step, 1)
            dve.wait_ge(r_den_step, 4)
            nc.vector.tensor_scalar(r_den[:, :, :], r_den[:, :, :], 1.0 - ALPHA, None, ALU.mult).then_inc(r_den_step, 1)
            dve.wait_ge(r_den_step, 5)

            def new_z():
                for c in range(Z_CHUNKS):
                    nc.vector.tensor_tensor(h_v[:, z_chunk(c), :].rearrange("p b (h d) -> p b h d", d=HD),
                                            agg[:, z_chunk(c), 0:DIM].rearrange("p b (h d) -> p b h d", d=HD),
                                            r_den[:, z_chunk(c), :].unsqueeze(3).broadcast_to([P, CHUNK_BLOCKS, HEADS, HD]),
                                            ALU.mult).then_inc(z_ready, 1)

            new_z()
            with dve.Fori(1, K_ITERS) as it:
                dve.wait_ge(agg_started, it * Z_CHUNKS)

                def messages(r, u):
                    dve.wait_ge(gathered[u], it * (BODIES * 16 * TILES) + r * (16 * TILES))
                    nc.vector.tensor_tensor(
                        msg[u % 2][:, :, 0:DIM].rearrange("p t (h d) -> p t h d", d=HD),
                        z_slot[u].rearrange("p t (h d) -> p t h d", d=HD),
                        group_weights(group0(r, u)).rearrange("p (t h) -> p t h", h=HEADS)
                        .unsqueeze(3).broadcast_to([P, TILES, HEADS, HD]), ALU.mult).then_inc(msg_ready, 1)
                    load_blocks(r, u)
                    aggregate(r, u, it * G + group1(r, u), DIM)

                def add_group(r, u):
                    add_last(r, u, it * G + group1(r, u), DIM)

                pipeline(dve, [(1, messages), (0, add_group)])
                dve.wait_ge(z_stored, it * (16 * Z_CHUNKS))
                add_extra(it * G + (G + 1), DIM)
                wait_next(dve, extra_added, extra_adds)
                new_z()
            dve.wait_ge(xh_loaded, 16)
            for c in range(Z_CHUNKS):
                dve.wait_ge(z_ready, (K_ITERS - 1) * Z_CHUNKS + c + 1)
                nc.vector.scalar_tensor_tensor(out=h_v[:, z_chunk(c), :], in0=h_v[:, z_chunk(c), :], scalar=0.0, in1=xh[:, z_chunk(c), :],
                                               op0=ALU.max, op1=ALU.add).then_inc(out_ready, 1)

        @block.tensor
        def _(pe):
            pe.wait_ge(w_loaded, 16 * 8)
            pe.wait_ge(consts_ready, 1)

            def products(j, n):
                pe.wait_ge(h_staged, j + 1)
                nc.tensor.transpose(ps_e[0][:, 0:P], h_stage[:, :], ident[:, :]).then_inc(h_turned, 1)
                pe.wait_ge(h_t_ready, j + 1)
                pe.wait_ge(kv_kept, j + 1)
                for half in range(2):
                    rows = slice(half * DIM, (half + 1) * DIM)
                    last = nc.tensor.matmul(ps_qkv[n][:, half, 0:3 * DIM], h_t[rows, :], w_qkv[rows, :], start=True, stop=True)
                last.then_inc(qkv_done, 1)

            for ch in range(KV_STORES):
                by_pair(pe, ch, products)

            pe.wait_ge(ranges_loaded, 16)
            pe.wait_ge(kv_kept, NB // 2 + 2)
            pe.sem_inc(e_done, U)
            pe.sem_inc(hot_used, 1)
            pe.sem_inc(max_psum, 1)
            pair = counter(pe, "pe_pair")
            submask = counter(pe, "pe_submask")
            group = counter(pe, "pe_group")
            extra = counter(pe, "pe_extra")

            def by_edge(r, u, width, parts):
                cols = TILES * width
                nc.tensor.matmul(ps_q[u % 2][:, 0:cols], zero_bf[:, 0:P], zero_bf[:, 0:cols], start=True, stop=True)
                lo, last_in = load_range(pe, r, u, BLOCKS)
                with pe.Fori(lo, last_in + 1) as b:
                    wait_next(pe, hot_ready, pair)
                    for t in range(TILES):
                        for part in range(PARTS):
                            last = nc.tensor.matmul(ps_q[u % 2][:, t * width:(t + 1) * width], hot_ne[:, t * P:(t + 1) * P],
                                                    parts[:, bass.ds(b, 1), part, :].rearrange("p a d -> p (a d)"),
                                                    start=False, stop=True, skip_group_check=True)
                    last.then_inc(hot_used, 1)

            def p1_e(r, u):
                pe.wait_ge(ea_loaded[u], r * 16)
                for j in range(TILES // 2):
                    last = nc.tensor.matmul(ps_e[u % 2][:, j * P:(j + 1) * P], ea_slot[u][:, j * P:(j + 1) * P], w_e[:, :], start=True, stop=True)
                last.then_inc(e_done, 1)

            def p1_q(r, u):
                by_edge(r, u, DIM, q_parts)

            def p1_turn(r, u):
                pe.wait_ge(lg_split, group1(r, u))
                for t in range(TILES):
                    last = nc.tensor.matmul(ps_t[2 * SUB:SROWS, t * P:(t + 1) * P], lg_parts[u % 2][:, t, :, :].rearrange("p c h -> p (c h)"),
                                            ident_bf[:, :], start=True, stop=True)
                last.then_inc(lgt_done, 1)

            def p1_spread(r, u):
                lo, last_in = load_range(pe, r, u, SUBS)
                with pe.Fori(lo, last_in + 1, 2):
                    n = pe.snap(submask)
                    pe.wait_ge(lgt_ready, group1(r, u))
                    pe.wait_ge(gmax_done, n)
                    pe.wait_ge(mask_ready, n)
                    pe.reg_add(submask, submask, 1)
                    for half in range(2):
                        last = nc.tensor.matmul(ps_b[:, half, :], spread_w[:, half, :], spread_in[:, :], start=True, stop=True)
                    last.then_inc(max_psum, 1)

            pipeline(pe, [(0, p1_spread), (1, p1_turn), (2, p1_e), (2, p1_q)])

            pe.wait_ge(m_sub_done, 1)
            subs = m_sub[:, 0:NSB].rearrange("p (b c) -> p c b", c=P // SUB)
            for h in range(HEADS):
                for c in range(P // SUB):
                    last = nc.tensor.matmul(ps_b[:, 0, h * NB:(h + 1) * NB], place[:, h, (3 - c) * SUB:(3 - c) * SUB + P], subs[:, c, :],
                                            start=c == 0, stop=c == P // SUB - 1)
            last.then_inc(m_moved, 1)

            def scatter_block(psum, hot, u, width):
                for t in range(TILES):
                    last = nc.tensor.matmul(psum[:, 0:width], hot[:, t, :], msg[u % 2][:, t, 0:width],
                                            start=t == 0, stop=t == TILES - 1)
                return last

            def scatter_group(r, u, width):
                lo, last_in = load_range(pe, r, u, BLOCKS)
                with pe.If(lo < last_in):
                    with pe.Fori(lo, last_in):
                        wait_next(pe, extra_ready, extra)
                        scatter_block(ps_e[0], hot_extra, u, width).then_inc(extra_psum, 1)
                wait_next(pe, hot_en_ready, group)
                scatter_block(ps_b[:, u % 2, :], hot_en[u % 2], u, width).then_inc(agg_psum, 1)

            def zero_extra():
                nc.tensor.matmul(ps_e[0][:, 0:AW], zero_bf[:, 0:P], zero_bf[:, 0:AW], start=True, stop=True).then_inc(extra_psum, 1)

            pe.wait_ge(m_ready, 1)
            zero_extra()
            def p2_max(r, u):
                pe.wait_ge(delta_ready, group1(r, u) - 2 + U)
                by_edge(r, u, HEADS, m_parts)

            pipeline(pe, [(1, lambda r, u: scatter_group(r, u, AW)), (3, p2_max)])

            with pe.Fori(1, K_ITERS) as it:
                pe.wait_ge(z_ready, it * Z_CHUNKS)
                zero_extra()
                pipeline(pe, [(0, lambda r, u: scatter_group(r, u, DIM))])


def kernel(x, src, dst, edge_attr_64, L0_gnn_Wq, L0_gnn_Wk, L0_gnn_Wv, L0_gnn_We):
    import concourse.bacc as bacc
    from concourse.bass_utils import run_bass_kernel_spmd

    def pad(a, rows, value=0):
        a = np.asarray(a)
        out = np.full((rows,) + a.shape[1:], value, a.dtype)
        out[:a.shape[0]] = a
        return out

    x_l = pad(x, NB * P).reshape(NB, P, DIM).transpose(1, 0, 2).reshape(P, NB * DIM)
    src_p, dst_p = pad(src, NT * P), pad(dst, NT * P, PAD_NODE)
    src_l = src_p.reshape(NT, P).T
    ea_t = pad(edge_attr_64, NT * P).reshape(G, TILES // 2, 2, P, DIM).transpose(0, 2, 4, 1, 3).reshape(G, P, GE // 2)
    arrays = {
        "x": x_l,
        "src": np.concatenate([src_l, src_l[:, :U * TILES]], axis=1),
        "dst": dst_p.reshape(NT, P).T,
        "dst_rows": dst_p.reshape(G, GE),
        "ea_t": ea_t,
        "wq": np.asarray(L0_gnn_Wq), "wk": np.asarray(L0_gnn_Wk), "wv": np.asarray(L0_gnn_Wv), "we": np.asarray(L0_gnn_We),
    }
    arrays = {f"in_{k}": np.ascontiguousarray(v) for k, v in arrays.items()}
    nc = bacc.Bacc("TRN2", target_bir_lowering=False, num_devices=1)
    aps = [nc.dram_tensor(k, v.shape, mybir.dt.from_np(v.dtype), kind="ExternalInput").ap() for k, v in arrays.items()]
    out = nc.dram_tensor("out_0", (P, NB * DIM), mybir.dt.float32, kind="ExternalOutput").ap()
    build_gnn(nc, *aps, out)
    res = run_bass_kernel_spmd(nc, [arrays], core_ids=[0])
    got = np.asarray(res.results[0]["out_0"]).reshape(P, NB, DIM).transpose(1, 0, 2).reshape(NB * P, DIM)
    return got[:N_NODES]
```
